# Optimizing a Trainium2 kernel written in Bass

```python
import numpy as np
import jax
import jax.numpy as jnp

def _softmax(x, axis=-1):
    return jax.nn.softmax(x, axis=axis)

def _gelu(x):
    return jax.nn.gelu(x, approximate=True)

def _silu(x):
    return jax.nn.silu(x)

def _sigmoid(x):
    return jax.nn.sigmoid(x)

def _layernorm(x, axis=-1, eps=1e-05):
    m = jnp.mean(x, axis=axis, keepdims=True)
    v = jnp.var(x, axis=axis, keepdims=True)
    return (x - m) / jnp.sqrt(v + eps)

def _scatter_add(tgt, idx, src, axis=0):
    return tgt.at[idx].add(src)

def _segment_sum(src, seg, n):
    return jax.ops.segment_sum(src, seg, n)
kernel_name = 'mk_sandwich_d1_jaxref_r8_89ddb2'

def setup_inputs(seed: int=0):
    np.random.seed(seed)
    _w = jnp.asarray

    def _L0_attn_setup():
        import jax, jax.numpy as jnp
        import numpy as np
        import math
        EPS_LN = 1e-05
        SCALE = 16.0

        def layer_norm(x, g):
            mean = jnp.mean(x, axis=-1, keepdims=True)
            var = jnp.var(x, axis=-1, keepdims=True)
            return (x - mean) * jax.lax.rsqrt(var + EPS_LN) * g

        def l2norm(t):
            n = jnp.linalg.norm(t, axis=-1, keepdims=True)
            return t / jnp.maximum(n, 1e-12)
        key = jax.random.key(seed)
        ks = jax.random.split(key, 4)
        b, n, dim, h, dh = (4, 256, 128, 8, 64)
        inner = h * dh
        x = jax.random.normal(ks[0], (b, n, dim), dtype=jnp.float32)
        Wq = jax.random.normal(ks[1], (dim, inner), dtype=jnp.float32) * dim ** (-0.5)
        Wkv = jax.random.normal(ks[2], (dim, 2 * dh), dtype=jnp.float32) * dim ** (-0.5)
        Wout = jax.random.normal(ks[3], (inner, dim), dtype=jnp.float32) * inner ** (-0.5)
        norm_g = jnp.ones((dim,), dtype=jnp.float32)
        out_norm_g = jnp.ones((dim,), dtype=jnp.float32)
        return {'x': x, 'norm_g': norm_g, 'Wq': Wq, 'Wkv': Wkv, 'Wout': Wout, 'out_norm_g': out_norm_g}
    _L0_attn_in = _L0_attn_setup()

    def _L0_ffn_setup():
        import jax, jax.numpy as jnp
        import numpy as np
        DIM = 128
        DEPTH = 2
        HEADS = 8
        DIM_HEAD = 64
        WINDOW = 64
        INNER = HEADS * DIM_HEAD
        HID = int(DIM * 4 * 2 / 3)
        B, N = (2, 1024)
        QK_SCALE = 8.0

        def shift_token(t):
            t1, t2 = jnp.split(t, 2, axis=-1)
            t2 = jnp.pad(t2, ((0, 0), (1, 0), (0, 0)))[:, :-1]
            return jnp.concatenate([t1, t2], axis=-1)

        def l2norm(t):
            return t / jnp.clip(jnp.linalg.norm(t, axis=-1, keepdims=True), 1e-12)

        def rotate_half(x):
            x1, x2 = jnp.split(x, 2, axis=-1)
            return jnp.concatenate([-x2, x1], axis=-1)

        def rotary_xpos(q, k):
            n = q.shape[-2]
            half_idx = jnp.arange(0, DIM_HEAD, 2, dtype=jnp.float32)
            inv_freq = 1.0 / 10000.0 ** (half_idx / DIM_HEAD)
            t = jnp.arange(n, dtype=jnp.float32)
            freqs = t[:, None] * inv_freq[None, :]
            freqs = jnp.concatenate([freqs, freqs], axis=-1)
            base = (half_idx + 0.4 * DIM_HEAD) / (1.4 * DIM_HEAD)
            power = (t - n // 2) / float(WINDOW // 2)
            scale = base[None, :] ** power[:, None]
            scale = jnp.concatenate([scale, scale], axis=-1)
            cos, sin = (jnp.cos(freqs), jnp.sin(freqs))
            q = q * cos * scale + rotate_half(q) * sin * scale
            k = k * cos / scale + rotate_half(k) * sin / scale
            return (q, k)

        def local_attention(q, k, v):
            b, h, n, d = q.shape
            w = n // WINDOW
            bq = q.reshape(b, h, w, WINDOW, d) * QK_SCALE
            bk = k.reshape(b, h, w, WINDOW, d)
            bv = v.reshape(b, h, w, WINDOW, d)

            def look_around(t):
                p = jnp.pad(t, ((0, 0), (0, 0), (1, 0), (0, 0), (0, 0)))
                return jnp.concatenate([p[:, :, :w], p[:, :, 1:]], axis=3)
            bk, bv = (look_around(bk), look_around(bv))
            bt = jnp.arange(n).reshape(w, WINDOW)
            btp = jnp.pad(bt, ((1, 0), (0, 0)), constant_values=-1)
            btk = jnp.concatenate([btp[:w], btp[1:]], axis=1)
            sim = jnp.einsum('bhwid,bhwjd->bhwij', bq, bk)
            i = bt[:, :, None]
            j = btk[:, None, :]
            mask = (i < j) | (i > j + WINDOW) | (j == -1)
            sim = jnp.where(mask, -jnp.finfo(sim.dtype).max, sim)
            attn = jax.nn.softmax(sim, axis=-1)
            out = jnp.einsum('bhwij,bhwjd->bhwid', attn, bv)
            return out.reshape(b, h, n, d)

        def _layer(x, wqkv, qs, ksc, wo, lg, lb, w1, b1, w2, b2):
            b, n, _ = x.shape
            h = shift_token(x)
            qkv = h @ wqkv
            q, k, v = jnp.split(qkv, 3, axis=-1)
            to_heads = lambda t: t.reshape(b, n, HEADS, DIM_HEAD).transpose(0, 2, 1, 3)
            q, k, v = (to_heads(q), to_heads(k), to_heads(v))
            q = l2norm(q) * qs
            k = l2norm(k) * ksc
            q, k = rotary_xpos(q, k)
            o = local_attention(q, k, v)
            o = o.transpose(0, 2, 1, 3).reshape(b, n, INNER)
            x = x + o @ wo
            h = shift_token(x)
            mu = h.mean(-1, keepdims=True)
            var = h.var(-1, keepdims=True)
            h = (h - mu) / jnp.sqrt(var + 1e-05) * lg + lb
            h = h @ w1 + b1
            a, g = jnp.split(h, 2, axis=-1)
            h = a * jax.nn.gelu(g, approximate=False)
            x = x + h @ w2 + b2
            return x
        key = jax.random.key(seed)
        ks = jax.random.split(key, 6)
        return {'x': jax.random.normal(ks[0], (B, N, DIM), jnp.float32), 'wqkv': jax.random.normal(ks[1], (DEPTH, DIM, 3 * INNER), jnp.float32) * 0.02, 'q_scale': jnp.ones((DEPTH, DIM_HEAD), jnp.float32), 'k_scale': jnp.ones((DEPTH, DIM_HEAD), jnp.float32), 'wo': jax.random.normal(ks[2], (DEPTH, INNER, DIM), jnp.float32) * 0.02, 'ln_g': jnp.ones((DEPTH, DIM), jnp.float32), 'ln_b': jnp.zeros((DEPTH, DIM), jnp.float32), 'w1': jax.random.normal(ks[3], (DEPTH, DIM, 2 * HID), jnp.float32) * 0.02, 'b1': jnp.zeros((DEPTH, 2 * HID), jnp.float32), 'w2': jax.random.normal(ks[4], (DEPTH, HID, DIM), jnp.float32) * 0.02, 'b2': jnp.zeros((DEPTH, DIM), jnp.float32)}
    _L0_ffn_in = _L0_ffn_setup()
    _d = {'L0_attn_x': _L0_attn_in['x'], 'L0_attn_norm_g': _L0_attn_in['norm_g'], 'L0_attn_Wq': _L0_attn_in['Wq'], 'L0_attn_Wkv': _L0_attn_in['Wkv'], 'L0_attn_Wout': _L0_attn_in['Wout'], 'L0_attn_out_norm_g': _L0_attn_in['out_norm_g'], 'L0_ffn_wqkv': _L0_ffn_in['wqkv'], 'L0_ffn_q_scale': _L0_ffn_in['q_scale'], 'L0_ffn_k_scale': _L0_ffn_in['k_scale'], 'L0_ffn_wo': _L0_ffn_in['wo'], 'L0_ffn_ln_g': _L0_ffn_in['ln_g'], 'L0_ffn_ln_b': _L0_ffn_in['ln_b'], 'L0_ffn_w1': _L0_ffn_in['w1'], 'L0_ffn_b1': _L0_ffn_in['b1'], 'L0_ffn_w2': _L0_ffn_in['w2'], 'L0_ffn_b2': _L0_ffn_in['b2']}
    _x0 = _d['L0_attn_x']
    _d['L0_attn_x'] = jax.random.normal(jax.random.fold_in(jax.random.key(seed), 1), (16, 256, 128), dtype=_x0.dtype)
    del _x0
    return _d

def reference(L0_attn_x, L0_attn_norm_g, L0_attn_Wq, L0_attn_Wkv, L0_attn_Wout, L0_attn_out_norm_g, L0_ffn_wqkv, L0_ffn_q_scale, L0_ffn_k_scale, L0_ffn_wo, L0_ffn_ln_g, L0_ffn_ln_b, L0_ffn_w1, L0_ffn_b1, L0_ffn_w2, L0_ffn_b2):

    def _L0_attn_ref(x, norm_g, Wq, Wkv, Wout, out_norm_g):
        import jax, jax.numpy as jnp
        import numpy as np
        import math
        EPS_LN = 1e-05
        SCALE = 16.0

        def layer_norm(x, g):
            mean = jnp.mean(x, axis=-1, keepdims=True)
            var = jnp.var(x, axis=-1, keepdims=True)
            return (x - mean) * jax.lax.rsqrt(var + EPS_LN) * g

        def l2norm(t):
            n = jnp.linalg.norm(t, axis=-1, keepdims=True)
            return t / jnp.maximum(n, 1e-12)
        b, n, dim = x.shape
        h = 8
        dh = Wkv.shape[-1] // 2
        xn = layer_norm(x, norm_g)
        q = xn @ Wq
        kv = xn @ Wkv
        k, v = (kv[..., :dh], kv[..., dh:])
        q = q.reshape(b, n, h, dh).transpose(0, 2, 1, 3)
        q = q * SCALE
        q = l2norm(q)
        k = l2norm(k)
        rs = math.sqrt(SCALE)
        q = q * rs
        k = k * rs
        sim = jnp.einsum('bhid,bjd->bhij', q, k)
        attn = jax.nn.softmax(sim.astype(jnp.float32), axis=-1).astype(sim.dtype)
        out = jnp.einsum('bhij,bjd->bhid', attn, v)
        out = out.transpose(0, 2, 1, 3).reshape(b, n, h * dh)
        out = out @ Wout
        return layer_norm(out, out_norm_g)

    def _L0_ffn_ref(x, wqkv, q_scale, k_scale, wo, ln_g, ln_b, w1, b1, w2, b2):
        import jax, jax.numpy as jnp
        import numpy as np
        DIM = 128
        DEPTH = 2
        HEADS = 8
        DIM_HEAD = 64
        WINDOW = 64
        INNER = HEADS * DIM_HEAD
        HID = int(DIM * 4 * 2 / 3)
        B, N = (2, 1024)
        QK_SCALE = 8.0

        def shift_token(t):
            t1, t2 = jnp.split(t, 2, axis=-1)
            t2 = jnp.pad(t2, ((0, 0), (1, 0), (0, 0)))[:, :-1]
            return jnp.concatenate([t1, t2], axis=-1)

        def l2norm(t):
            return t / jnp.clip(jnp.linalg.norm(t, axis=-1, keepdims=True), 1e-12)

        def rotate_half(x):
            x1, x2 = jnp.split(x, 2, axis=-1)
            return jnp.concatenate([-x2, x1], axis=-1)

        def rotary_xpos(q, k):
            n = q.shape[-2]
            half_idx = jnp.arange(0, DIM_HEAD, 2, dtype=jnp.float32)
            inv_freq = 1.0 / 10000.0 ** (half_idx / DIM_HEAD)
            t = jnp.arange(n, dtype=jnp.float32)
            freqs = t[:, None] * inv_freq[None, :]
            freqs = jnp.concatenate([freqs, freqs], axis=-1)
            base = (half_idx + 0.4 * DIM_HEAD) / (1.4 * DIM_HEAD)
            power = (t - n // 2) / float(WINDOW // 2)
            scale = base[None, :] ** power[:, None]
            scale = jnp.concatenate([scale, scale], axis=-1)
            cos, sin = (jnp.cos(freqs), jnp.sin(freqs))
            q = q * cos * scale + rotate_half(q) * sin * scale
            k = k * cos / scale + rotate_half(k) * sin / scale
            return (q, k)

        def local_attention(q, k, v):
            b, h, n, d = q.shape
            w = n // WINDOW
            bq = q.reshape(b, h, w, WINDOW, d) * QK_SCALE
            bk = k.reshape(b, h, w, WINDOW, d)
            bv = v.reshape(b, h, w, WINDOW, d)

            def look_around(t):
                p = jnp.pad(t, ((0, 0), (0, 0), (1, 0), (0, 0), (0, 0)))
                return jnp.concatenate([p[:, :, :w], p[:, :, 1:]], axis=3)
            bk, bv = (look_around(bk), look_around(bv))
            bt = jnp.arange(n).reshape(w, WINDOW)
            btp = jnp.pad(bt, ((1, 0), (0, 0)), constant_values=-1)
            btk = jnp.concatenate([btp[:w], btp[1:]], axis=1)
            sim = jnp.einsum('bhwid,bhwjd->bhwij', bq, bk)
            i = bt[:, :, None]
            j = btk[:, None, :]
            mask = (i < j) | (i > j + WINDOW) | (j == -1)
            sim = jnp.where(mask, -jnp.finfo(sim.dtype).max, sim)
            attn = jax.nn.softmax(sim, axis=-1)
            out = jnp.einsum('bhwij,bhwjd->bhwid', attn, bv)
            return out.reshape(b, h, n, d)

        def _layer(x, wqkv, qs, ksc, wo, lg, lb, w1, b1, w2, b2):
            b, n, _ = x.shape
            h = shift_token(x)
            qkv = h @ wqkv
            q, k, v = jnp.split(qkv, 3, axis=-1)
            to_heads = lambda t: t.reshape(b, n, HEADS, DIM_HEAD).transpose(0, 2, 1, 3)
            q, k, v = (to_heads(q), to_heads(k), to_heads(v))
            q = l2norm(q) * qs
            k = l2norm(k) * ksc
            q, k = rotary_xpos(q, k)
            o = local_attention(q, k, v)
            o = o.transpose(0, 2, 1, 3).reshape(b, n, INNER)
            x = x + o @ wo
            h = shift_token(x)
            mu = h.mean(-1, keepdims=True)
            var = h.var(-1, keepdims=True)
            h = (h - mu) / jnp.sqrt(var + 1e-05) * lg + lb
            h = h @ w1 + b1
            a, g = jnp.split(h, 2, axis=-1)
            h = a * jax.nn.gelu(g, approximate=False)
            x = x + h @ w2 + b2
            return x
        for l in range(DEPTH):
            x = _layer(x, wqkv[l], q_scale[l], k_scale[l], wo[l], ln_g[l], ln_b[l], w1[l], b1[l], w2[l], b2[l])
        return x
    x = L0_attn_x
    x = x + _layernorm(_L0_attn_ref(_layernorm(x, axis=-1), L0_attn_norm_g, L0_attn_Wq, L0_attn_Wkv, L0_attn_Wout, L0_attn_out_norm_g), axis=-1)
    x = x + _layernorm(_L0_ffn_ref(_layernorm(x, axis=-1), L0_ffn_wqkv, L0_ffn_q_scale, L0_ffn_k_scale, L0_ffn_wo, L0_ffn_ln_g, L0_ffn_ln_b, L0_ffn_w1, L0_ffn_b1, L0_ffn_w2, L0_ffn_b2), axis=-1)
    return x

_drawn_inputs = setup_inputs


def setup_inputs(seed=0):
    import zlib

    import numpy as np

    out = dict(_drawn_inputs(seed))
    spreads = {'L0_attn_norm_g': (1.0, 0.2),
     'L0_attn_out_norm_g': (1.0, 0.2),
     'L0_ffn_q_scale': (1.0, 0.6),
     'L0_ffn_k_scale': (1.0, 0.6),
     'L0_ffn_ln_g': (1.0, 0.6),
     'L0_ffn_ln_b': (0.0, 0.8),
     'L0_ffn_b1': (0.0, 0.8),
     'L0_ffn_b2': (0.0, 0.8)}
    factors = {'L0_ffn_wqkv': 3.51, 'L0_ffn_wo': 3.52, 'L0_ffn_w1': 7.571, 'L0_ffn_w2': 7.472}
    for name, (base, spread) in spreads.items():
        noise = np.random.default_rng([zlib.crc32(name.encode()), seed]).standard_normal(out[name].shape)
        drawn = base * np.exp(spread * noise) if base else spread * noise
        out[name] = jnp.asarray(drawn.astype(out[name].dtype))
    for name, factor in factors.items():
        out[name] = (out[name] * factor).astype(out[name].dtype)
    return out
```

```python
from contextlib import ExitStack

import numpy as np

import concourse.bass as bass
from concourse import mybir
from concourse.alu_op_type import AluOpType as ALU

F32 = mybir.dt.float32
BF16 = mybir.dt.bfloat16
ACT = mybir.ActivationFunctionType
AX_X = mybir.AxisListType.X

P = 128
TOK = 256
TILES = TOK // P
DIM = 128
HEADS = 8
DH = 64
INNER = HEADS * DH
PAIRS = HEADS // 2
WINDOW = 64
DEPTH = 2
HID = int(DIM * 4 * 2 / 3)
HID_CHUNKS = [(c, min(P, HID - c)) for c in range(0, HID, P)]
NCH = len(HID_CHUNKS)
HID_LAST = HID_CHUNKS[-1][1]
EPS = 1e-5
QK_SCALE = 8.0
SIM_SCALE = 16.0
NEG = -1e30
STREAMS = 2
DONE = object()
LOADS = 9 + DEPTH * (8 + 3 * NCH)
PRESETS = 1 + 5 * STREAMS
LINKS = 52
UNITS = TILES * PAIRS


def shape_constants():
    half = np.arange(0, DH, 2, dtype=np.float32)
    inv_freq = (1.0 / np.float32(10000.0) ** (half / np.float32(DH))).astype(np.float32)
    t = np.arange(TOK, dtype=np.float32)
    freqs = t[:, None] * inv_freq[None, :]
    freqs = np.concatenate([freqs, freqs], axis=-1)
    base = (half + np.float32(0.4 * DH)) / np.float32(1.4 * DH)
    power = (t - TOK // 2) / np.float32(WINDOW // 2)
    scale = base[None, :] ** power[:, None]
    scale = np.concatenate([scale, scale], axis=-1)
    cos, sin = np.cos(freqs), np.sin(freqs)
    sign = np.where(np.arange(DH) < DH // 2, -1.0, 1.0).astype(np.float32)
    rot = np.stack([np.stack([cos * scale * QK_SCALE, sign * sin * scale * QK_SCALE], 1),
                    np.stack([cos / scale, sign * sin / scale], 1)], 1).astype(np.float32)
    rot = rot.reshape(TILES, P, 2, 2, DH).transpose(1, 0, 2, 3, 4)
    i, j = np.arange(TOK)[:, None], np.arange(TOK)[None, :]
    mask = np.where((i < j) | (i > j + WINDOW), NEG, 0.0).astype(np.float32)
    mask = mask.reshape(TILES, P, TOK).transpose(1, 0, 2)
    shift = np.zeros((P, 2, P), np.float32)
    shift[np.arange(P - 1), 0, np.arange(1, P)] = 1.0
    shift[P - 1, 1, 0] = 1.0
    return {
        "rot": np.ascontiguousarray(rot.reshape(P, -1)),
        "mask": np.ascontiguousarray(mask.reshape(P, -1)),
        "ident": np.eye(P, dtype=np.float32),
        "shift": shift.reshape(P, -1),
    }


def sandwich_kernel(nc: bass.Bass, x, norm_g, Wq, Wkv, Wout, out_norm_g, wqkv, q_scale, k_scale, wo,
                    ln_g, ln_b, w1, b1, w2, b2, rot_c, mask_c, ident_c, shift_c, out):
    B = x.shape[0]
    ROUNDS = B // STREAMS

    with ExitStack() as ctx:
        def sb(name, shape, dt=F32):
            return ctx.enter_context(nc.sbuf_tensor(name, shape, dt))

        def sem(name):
            return ctx.enter_context(nc.semaphore(name))

        def per_stream(make):
            return [make(s) for s in range(STREAMS)]

        ident = sb("ident", [P, P])
        identb = sb("identb", [P, P], BF16)
        shift = sb("shift", [P, 2, P])
        maskf = sb("maskf", [P, TILES, TOK])
        maskb = sb("maskb", [P, TILES, TOK], BF16)
        rot = sb("rot", [P, TILES, 2, 2, DH])
        qks = sb("qks", [P, DEPTH, 2, DH])
        tab = [sb(f"tab{l}", [P, TILES, 2, 2, DH]) for l in range(DEPTH)]
        ng = sb("ng", [P, 1])
        outg = sb("outg", [P, DIM])
        wq_s = sb("wq_s", [P, INNER])
        wkv_s = sb("wkv_s", [P, 2 * DH])
        wout_s = sb("wout_s", [P, PAIRS, DIM])
        wqkv_s = [sb(f"wqkv_s{l}", [P, 3 * INNER]) for l in range(DEPTH)]
        wo_s = [sb(f"wo_s{l}", [P, PAIRS, DIM]) for l in range(DEPTH)]
        w1_raw = [sb(f"w1_raw{l}", [P, 2 * HID]) for l in range(DEPTH)]
        w1_s = [sb(f"w1_s{l}", [P, 2 * HID]) for l in range(DEPTH)]
        w2_s = [sb(f"w2_s{l}", [P, NCH, DIM]) for l in range(DEPTH)]
        lng = sb("lng", [P, DEPTH])
        lnb = sb("lnb", [P, DEPTH])
        b1c = sb("b1c", [P, DEPTH, 2, NCH])
        b1f = sb("b1f", [P, DEPTH, 2, NCH])
        halfpow = sb("halfpow", [P, 2 * 2 * HEADS + 4])

        xin = per_stream(lambda s: sb(f"xin{s}", [P, TILES, DIM]))
        x1 = per_stream(lambda s: sb(f"x1_{s}", [P, TILES, DIM]))
        y = per_stream(lambda s: sb(f"y{s}", [P, TILES, DIM]))
        z = per_stream(lambda s: sb(f"z{s}", [P, TILES, DIM]))
        h = per_stream(lambda s: sb(f"h{s}", [P, TILES, DIM]))
        fin = per_stream(lambda s: sb(f"fin{s}", [P, TILES, DIM]))
        st = per_stream(lambda s: sb(f"st{s}", [P, TILES, 2, 6]))
        aside = per_stream(lambda s: sb(f"aside{s}", [P, 1]))
        mv = per_stream(lambda s: sb(f"mv{s}", [P, TILES, 2]))
        arg = per_stream(lambda s: sb(f"arg{s}", [P, TILES]))
        rstd = per_stream(lambda s: sb(f"rstd{s}", [P, TILES]))
        actT = per_stream(lambda s: sb(f"actT{s}", [P, TOK + 1]))
        shT = per_stream(lambda s: sb(f"shT{s}", [P, TOK + 1]))
        sq = per_stream(lambda s: sb(f"sq{s}", [P, 2, 2 * INNER]))
        ss = per_stream(lambda s: sb(f"ss{s}", [P, TILES, 2 * HEADS]))
        rn = per_stream(lambda s: sb(f"rn{s}", [P, TILES, 2 * HEADS]))
        qk = per_stream(lambda s: sb(f"qk{s}", [P, TILES, 2 * INNER]))
        t1 = per_stream(lambda s: sb(f"t1_{s}", [P, 2 * INNER]))
        t2 = per_stream(lambda s: sb(f"t2_{s}", [P, 2 * INNER]))
        qT = per_stream(lambda s: sb(f"qT{s}", [P, PAIRS, TOK]))
        kT = per_stream(lambda s: sb(f"kT{s}", [P, PAIRS, TOK]))
        v1 = per_stream(lambda s: sb(f"v1_{s}", [P, TILES, DH + 1]))
        v8 = per_stream(lambda s: sb(f"v8_{s}", [P, TILES, INNER]))
        pb = per_stream(lambda s: [sb(f"pb{s}_{b}", [P, 2, TOK]) for b in range(4)])
        pT = per_stream(lambda s: [sb(f"pT{s}_{b}", [P, 2, 2, P]) for b in range(2)])
        nmax = per_stream(lambda s: sb(f"nmax{s}", [P, UNITS, 2]))
        psm = per_stream(lambda s: sb(f"psm{s}", [P, TILES, HEADS]))
        rsm = per_stream(lambda s: sb(f"rsm{s}", [P, TILES, HEADS]))
        o = per_stream(lambda s: sb(f"o{s}", [P, TILES, INNER]))
        oT = per_stream(lambda s: sb(f"oT{s}", [P, PAIRS, TOK]))
        gate = per_stream(lambda s: sb(f"gate{s}", [P, NCH, TOK]))
        hid = per_stream(lambda s: sb(f"hid{s}", [P, NCH, TOK]))

        ps = per_stream(lambda s: ctx.enter_context(nc.psum_tensor(f"ps{s}", [P, 4, 512], F32)))

        s_w = sem("weights_loaded")
        s_wa = sem("weights_ready_dve")
        s_wp = sem("bias_product_ready")
        s_init = sem("presets_done")
        s_ld = [sem(f"x_loaded{s}") for s in range(STREAMS)]
        s_st = [sem(f"out_stored{s}") for s in range(STREAMS)]

        class Signal:

            def __init__(self, name, per):
                self.per = per
                self.sems = [sem(f"{name}{s}") for s in range(STREAMS)]

            def __getitem__(self, s):
                return self.sems[s]

            def at(self, k, n):
                return k * self.per + (n + 1)

        xfree = Signal("x_consumed", 1)
        own = Signal("dve_own", LINKS)
        var_ready = Signal("variance_ready", 5 + DEPTH)
        rstd_ready = Signal("rstd_ready", 5 + DEPTH)
        y_ready = Signal("normed_ready", 1)
        act_ps = Signal("actT_in_psum", 1 + 2 * DEPTH)
        act_sb = Signal("actT_in_sbuf", 1 + 2 * DEPTH)
        aq_ps = Signal("a_qkv_in_psum", 3)
        aq_sq = Signal("a_squares_ready", 3)
        av_sb = Signal("a_v_ready", 1)
        ss_ready = Signal("norms_squared_ready", 1 + TILES * DEPTH)
        rn_ready = Signal("inverse_norms_ready", 1 + TILES * DEPTH)
        aqk_n = Signal("a_qk_normed", 3)
        aqT_ps = Signal("a_qkT_in_psum", 3)
        aqT_sb = Signal("a_qkT_in_sbuf", 3)
        as_ps = Signal("a_scores_in_psum", HEADS)
        ap_sb = Signal("a_probs_ready", HEADS)
        ao_ps = Signal("a_head_out_in_psum", HEADS)
        ao_sb = Signal("a_out_normed", 2)
        oT_ps = Signal("oT_in_psum", TILES * (1 + DEPTH))
        oT_sb = Signal("oT_in_sbuf", TILES * (1 + DEPTH))
        proj_ps = Signal("out_projection_in_psum", 1 + DEPTH)
        h_ready = Signal("residual_ready", 1 + DEPTH)
        h_mid = Signal("residual_after_attention", DEPTH)
        qk_ps = Signal("qk_in_psum", TILES * DEPTH)
        v_ps = Signal("v_in_psum", TILES * DEPTH)
        v_sb = Signal("v_in_sbuf", TILES * DEPTH)
        qk_sq = Signal("qk_squares_ready", 2 * TILES * DEPTH)
        qk_t = Signal("rotary_products_ready", TILES * DEPTH)
        qk_rot = Signal("rotary_sum_ready", TILES * DEPTH)
        qk_n = Signal("qk_rotated_normed", TILES * DEPTH)
        qkT_ps = Signal("qkT_in_psum", 2 * TILES * DEPTH)
        qkT_sb = Signal("qkT_in_sbuf", 2 * TILES * DEPTH)
        s_ps = Signal("scores_in_psum", UNITS * DEPTH)
        mx_ready = Signal("negated_max_ready", UNITS * DEPTH)
        p_sb = Signal("probs_ready", UNITS * DEPTH)
        pT_ps = Signal("probsT_in_psum", UNITS * DEPTH)
        pT_sb = Signal("probsT_in_sbuf", UNITS * DEPTH)
        pv_ps = Signal("head_out_in_psum", UNITS * DEPTH)
        o_sb = Signal("out_normed", TILES * DEPTH)
        sh_ps = Signal("shifted_half_in_psum", DEPTH)
        hn_ready = Signal("shifted_normed_ready", DEPTH)
        f1_ps = Signal("hidden_in_psum", NCH * DEPTH)
        gate_sb = Signal("gate_ready", NCH * DEPTH)
        hid_sb = Signal("hidden_ready", NCH * DEPTH)
        f2_ps = Signal("ffn_out_in_psum", DEPTH)
        fin_ready = Signal("result_ready", 1)

        def rows(n):
            return slice(64 * n, 64 * n + 64)

        def keys(t):
            return slice(max(t * P - WINDOW, 0), (t + 1) * P)

        def unit(u):
            t, n = divmod(u, PAIRS)
            return t, [4 * (n // 2) + n % 2, 4 * (n // 2) + 2 + n % 2]

        def blocks(t):
            return range(t + 1)

        x_v = x.rearrange("b (t p) d -> b p t d", p=P)
        out_v = out.rearrange("b (t p) d -> b p t d", p=P)

        block = ctx.enter_context(nc.Block())

        @block.sync
        def _(sp):
            loads = [0]

            def load(dst, src):
                sp.dma_start(dst, src).then_inc(s_w, 16)
                loads[0] += 1

            for s in range(STREAMS):
                sp.dma_start(xin[s][:, :, :], x_v[s]).then_inc(s_ld[s], 16)
                sp.sem_inc(s_st[s], 16)
            load(ident[:, :], ident_c)
            load(ng[:, :], norm_g.rearrange("(p a) -> p a", a=1))
            load(wq_s[:, :], Wq)
            load(wkv_s[:, :], Wkv)
            load(wout_s[:, :, :], Wout.rearrange("(c p) n -> p c n", p=P))
            load(outg[:, :], out_norm_g.partition_broadcast(P))
            load(shift[:, :, :], shift_c.rearrange("p (a n) -> p a n", a=2))
            load(maskf[:, :, :], mask_c.rearrange("p (a n) -> p a n", a=TILES))
            load(rot[:, :, :, :, :], rot_c.rearrange("p (t a b d) -> p t a b d", t=TILES, a=2, b=2))
            for l in range(DEPTH):
                load(wqkv_s[l][:, :], wqkv[l])
                load(qks[:, l, 0, :], q_scale[l].partition_broadcast(P))
                load(qks[:, l, 1, :], k_scale[l].partition_broadcast(P))
                load(wo_s[l][:, :, :], wo[l].rearrange("(c p) n -> p c n", p=P))
                load(lng[:, l:l + 1], ln_g[l].rearrange("(p a) -> p a", a=1))
                load(lnb[:, l:l + 1], ln_b[l].rearrange("(p a) -> p a", a=1))
                load(w1_raw[l][:, :], w1[l])
                for c, (c0, n) in enumerate(HID_CHUNKS):
                    for part in range(2):
                        load(b1c[0:n, l, part, c:c + 1],
                             b1[l, part * HID + c0:part * HID + c0 + n].rearrange("(p a) -> p a", a=1))
                    load(w2_s[l][0:n, c, :], w2[l, c0:c0 + n, :])
                load(w2_s[l][HID_LAST:HID_LAST + 1, NCH - 1, :], b2[l:l + 1, :])
            assert loads[0] == LOADS, loads[0]

            def store(s, k, b):
                sp.wait_ge(fin_ready[s], fin_ready.at(k, 0))
                sp.dma_start(out_v[b], fin[s][:, :, :]).then_inc(s_st[s], 16)

            with sp.Fori(0, ROUNDS - 1) as k:
                for s in range(STREAMS):
                    sp.wait_ge(xfree[s], xfree.at(k, 0))
                    sp.dma_start(xin[s][:, :, :], x_v[(k + 1) * STREAMS + s]).then_inc(s_ld[s], 16)
                for s in range(STREAMS):
                    store(s, k, k * STREAMS + s)
            for s in range(STREAMS):
                store(s, ROUNDS - 1, (ROUNDS - 1) * STREAMS + s)
            for s in range(STREAMS):
                sp.wait_ge(s_st[s], 16 * (ROUNDS + 1))

        @block.gpsimd
        def _(pool):
            pool.memset(halfpow[:, :], -0.5).then_inc(s_init, 1)
            for s in range(STREAMS):
                pool.memset(v1[s][:, :, DH:DH + 1], 1.0).then_inc(s_init, 1)
                pool.memset(shT[s][:, :], 0.0).then_inc(s_init, 1)
                pool.memset(hid[s][:, :, :], 1.0).then_inc(s_init, 1)
                for b in range(2, 4):
                    pool.memset(pb[s][b][:, :, 0:WINDOW], 0.0).then_inc(s_init, 1)
            pool.wait_ge(s_init, PRESETS)

            def batch(s, k):
                def layer_rstd(n):
                    pool.wait_ge(var_ready[s], var_ready.at(k, n))
                    pool.tensor_tensor(rstd[s][:, :], arg[s][:, :], halfpow[:, 0:TILES],
                                                       ALU.pow).then_inc(rstd_ready[s], 1)

                layer_rstd(0)
                yield
                pool.wait_ge(ss_ready[s], ss_ready.at(k, 0))
                n = TILES * (HEADS + 1)
                pool.tensor_tensor(
                    rn[s][:, :, :].rearrange("p t h -> p (t h)")[:, 0:n],
                    ss[s][:, :, :].rearrange("p t h -> p (t h)")[:, 0:n], halfpow[:, 0:n], ALU.pow).then_inc(rn_ready[s], 1)
                yield
                for n in range(1, 4):
                    layer_rstd(n)
                    yield
                for l in range(DEPTH):
                    for t in range(TILES):
                        j = l * TILES + t
                        pool.wait_ge(ss_ready[s], ss_ready.at(k, 1 + j))
                        pool.tensor_tensor(rn[s][:, t, :], ss[s][:, t, :],
                                                         halfpow[:, 0:2 * HEADS], ALU.pow).then_inc(rn_ready[s], 1)
                        yield
                    layer_rstd(4 + l)
                    yield
                layer_rstd(4 + DEPTH)
                yield

            with pool.Fori(0, ROUNDS) as k:
                interleave([batch(s, k) for s in range(STREAMS)])

        @block.scalar
        def _(act):
            act.wait_ge(s_init, PRESETS)

            def batch(s, k):
                B4 = ps[s]
                copy, square = ACT.Copy, ACT.Square
                act.wait_ge(act_ps[s], act_ps.at(k, 0))
                act.activation(actT[s][:, 0:TOK], B4[:, 3, 0:TOK], copy).then_inc(act_sb[s], 1)
                yield
                for t in range(TILES):
                    act.wait_ge(aq_ps[s], aq_ps.at(k, t))
                    act.activation(sq[s][:, t, 0:INNER], B4[:, t, :], square).then_inc(aq_sq[s], 1)
                act.wait_ge(aq_ps[s], aq_ps.at(k, 2))
                kv = B4[:, 2, 0:TILES * 2 * DH].rearrange("p (t n) -> p t n", t=TILES)
                act.activation(sq[s][:, :, INNER:INNER + DH], kv[:, :, 0:DH], square).then_inc(aq_sq[s], 1)
                act.activation(v1[s][:, :, 0:DH], kv[:, :, DH:2 * DH], copy).then_inc(av_sb[s], 1)
                yield
                for t, bank in ((0, 3), (1, 0)):
                    act.wait_ge(aqT_ps[s], aqT_ps.at(k, t))
                    act.activation(qT[s][:, :, t * P:(t + 1) * P],
                                               B4[:, bank, :].rearrange("p (c n) -> p c n", c=PAIRS), copy).then_inc(aqT_sb[s], 1)
                act.wait_ge(aqT_ps[s], aqT_ps.at(k, 2))
                act.activation(kT[s][:, 0, :], B4[:, 1, 0:TOK], copy).then_inc(aqT_sb[s], 1)
                yield
                for hd in range(HEADS):
                    act.wait_ge(as_ps[s], as_ps.at(k, hd))
                    if hd >= 2:
                        act.wait_ge(ao_ps[s], ao_ps.at(k, hd - 2))
                    act.activation(pb[s][hd % 2][:, :, :].rearrange("p a n -> p (a n)"),
                                              B4[:, hd % 2, :], ACT.Exp, scale=SIM_SCALE).then_inc(ap_sb[s], 1)
                    yield

                def out_T(n0):
                    for t in range(TILES):
                        act.wait_ge(oT_ps[s], oT_ps.at(k, n0 + t))
                        act.activation(oT[s][:, :, t * P:(t + 1) * P],
                                                  B4[:, t, :].rearrange("p (c n) -> p c n", c=PAIRS), copy).then_inc(oT_sb[s], 1)
                    
                out_T(0)
                yield
                for l in range(DEPTH):
                    act.wait_ge(act_ps[s], act_ps.at(k, 1 + 2 * l))
                    act.activation(shT[s][0:64, 0:TOK], B4[0:64, 3, 0:TOK], copy)
                    act.activation(shT[s][64:128, 1:TOK + 1], B4[64:128, 3, 0:TOK], copy).then_inc(act_sb[s], 1)
                    yield
                    for t in range(TILES):
                        j = l * TILES + t
                        act.wait_ge(qk_ps[s], qk_ps.at(k, j))
                        for part in range(2):
                            act.activation(sq[s][:, t, part * INNER:(part + 1) * INNER],
                                                      B4[:, part, :], square).then_inc(qk_sq[s], 1)
                        act.wait_ge(v_ps[s], v_ps.at(k, j))
                        act.activation(v8[s][:, t, :], B4[:, 2 + t, :], copy).then_inc(v_sb[s], 1)
                        yield
                    for t in range(TILES):
                        for part, dst in ((0, qT), (1, kT)):
                            j = (l * TILES + t) * 2 + part
                            bank = (2 if t == 0 else 0) + part
                            act.wait_ge(qkT_ps[s], qkT_ps.at(k, j))
                            act.activation(
                                dst[s][:, :, t * P:(t + 1) * P],
                                B4[:, bank, :].rearrange("p (c n) -> p c n", c=PAIRS), copy).then_inc(qkT_sb[s], 1)
                        yield
                    for u in range(UNITS):
                        t, heads = unit(u)
                        j = l * UNITS + u
                        act.wait_ge(mx_ready[s], mx_ready.at(k, j))
                        if u >= 2:
                            act.wait_ge(pT_ps[s], pT_ps.at(k, j - 2))
                        for e, hd in enumerate(heads):
                            ins = act.activation(pb[s][2 * t + u % 2][:, e, keys(t)],
                                                 B4[:, u % 2, :].rearrange("p (e n) -> p e n", e=2)[:, e, keys(t)],
                                                 ACT.Exp, bias=nmax[s][:, u, e:e + 1],
                                                 accum_out=psm[s][:, t, hd:hd + 1])
                        ins.then_inc(p_sb[s], 1)
                        yield
                    out_T(TILES * (1 + l))
                    yield
                    act.wait_ge(act_ps[s], act_ps.at(k, 2 + 2 * l))
                    act.activation(actT[s][:, 0:TOK], B4[:, 0, 0:TOK], copy).then_inc(act_sb[s], 1)
                    yield
                    for c, (_, n) in enumerate(HID_CHUNKS):
                        act.wait_ge(f1_ps[s], f1_ps.at(k, l * NCH + c))
                        act.activation(gate[s][0:n, c, :], B4[0:n, 1 + c, TOK:2 * TOK], ACT.Gelu,
                                                    bias=b1f[0:n, l, 1, c:c + 1]).then_inc(gate_sb[s], 1)
                    yield

            act.wait_ge(s_wa, 2)
            with act.Fori(0, ROUNDS) as k:
                interleave([batch(s, k) for s in range(STREAMS)])

        @block.vector
        def _(dve):
            dve.wait_ge(s_w, 16 * LOADS)
            dve.tensor_scalar(wq_s[:, :], wq_s[:, :], ng[:, 0:1], None, ALU.mult)
            dve.tensor_scalar(wkv_s[:, :], wkv_s[:, :], ng[:, 0:1], None, ALU.mult)
            dve.tensor_copy(identb[:, :], ident[:, :])
            dve.tensor_copy(maskb[:, :, :], maskf[:, :, :])
            for l in range(DEPTH):
                dve.tensor_scalar(w1_s[l][:, :], w1_raw[l][:, :], lng[:, l:l + 1], None, ALU.mult)
                for t in range(TILES):
                    for part in range(2):
                        qs = qks[:, l, part, :]
                        dve.tensor_tensor(tab[l][:, t, part, 0, :], rot[:, t, part, 0, :], qs, ALU.mult)
                        ins = dve.tensor_tensor(
                            tab[l][:, t, part, 1, :].rearrange("p (a d) -> p a d", a=2),
                            rot[:, t, part, 1, :].rearrange("p (a d) -> p a d", a=2),
                            qs.rearrange("p (a d) -> p a d", a=2)[:, ::-1, :], ALU.mult)
            ins.then_inc(s_wa, 1)
            dve.wait_ge(s_wp, 1)
            for l in range(DEPTH):
                for part in range(2):
                    for c, (_, n) in enumerate(HID_CHUNKS):
                        col = (l * 2 + part) * NCH + c
                        ins = dve.tensor_tensor(b1f[0:n, l, part, c:c + 1], b1c[0:n, l, part, c:c + 1],
                                                ps[0][0:n, 0, col:col + 1], ALU.add)
            ins.then_inc(s_wa, 1)
            dve.wait_ge(s_init, PRESETS)

            def batch(s, k):
                B4 = ps[s]
                links = [0]

                def link(*instructions):
                    for ins in instructions:
                        ins.then_inc(own[s], 1)
                        links[0] += 1
                    dve.wait_ge(own[s], own.at(k, links[0] - 1))

                def stats(parts):
                    link(*[dve.bn_stats(st[s][:, t, a, :], part)
                           for t in range(TILES) for a, part in enumerate(parts(t))])
                    dve.memset(aside[s][:, :], 0.0)
                    link(*[dve.bn_aggr(mv[s][:, t, :], st[s][:, t, 0:len(parts(t)), :])
                           for t in range(TILES)])

                def inverse_std(n, times=1.0, plus=EPS):
                    dve.tensor_scalar(arg[s][:, :], mv[s][:, :, 1], times, plus,
                                                     ALU.mult, ALU.add).then_inc(var_ready[s], 1)
                    yield
                    dve.wait_ge(rstd_ready[s], rstd_ready.at(k, n))

                def normed(dst, src, t):
                    return dve.tensor_scalar(dst, src, mv[s][:, t, 0:1], rstd[s][:, t:t + 1],
                                             ALU.subtract, ALU.mult)

                dve.wait_ge(s_ld[s], k * 16 + 16)
                stats(lambda t: [xin[s][:, t, :]])
                yield from inverse_std(0, 1.0 + EPS, EPS * EPS)
                for t in range(TILES):
                    ins = normed(y[s][:, t, :], xin[s][:, t, :], t)
                ins.then_inc(y_ready[s], 1)
                yield
                dve.wait_ge(aq_sq[s], aq_sq.at(k, 2))
                ssv = ss[s][:, :, :].rearrange("p t h -> p (t h)")[:, 0:TILES * (HEADS + 1)]\
                    .rearrange("p (t h) -> p t h", t=TILES)
                rnv = rn[s][:, :, :].rearrange("p t h -> p (t h)")[:, 0:TILES * (HEADS + 1)]\
                    .rearrange("p (t h) -> p t h", t=TILES)
                link(dve.tensor_reduce(ssv, sq[s][:, :, 0:INNER + DH].rearrange("p t (h d) -> p t h d", d=DH),
                                       AX_X, ALU.add))
                dve.tensor_scalar(ssv[:, :, 0:HEADS], ssv[:, :, 0:HEADS], (1e-12 / SIM_SCALE) ** 2, None, ALU.max)
                dve.tensor_scalar(ssv[:, :, HEADS:HEADS + 1], ssv[:, :, HEADS:HEADS + 1],
                                                1e-24, None, ALU.max).then_inc(ss_ready[s], 1)
                yield
                dve.wait_ge(rn_ready[s], rn_ready.at(k, 0))
                for t in range(TILES):
                    dve.tensor_tensor(
                        qk[s][:, t, 0:INNER].rearrange("p (h d) -> p h d", d=DH),
                        B4[:, t, :].rearrange("p (h d) -> p h d", d=DH),
                        rnv[:, t, 0:HEADS].unsqueeze(2).broadcast_to([P, HEADS, DH]), ALU.mult).then_inc(aqk_n[s], 1)
                dve.wait_ge(av_sb[s], av_sb.at(k, 0))
                for t in range(TILES):
                    ins = dve.tensor_scalar(
                        qk[s][:, t, INNER:INNER + P].rearrange("p (a d) -> p a d", a=2),
                        B4[:, 2, t * 2 * DH:t * 2 * DH + DH].unsqueeze(1).broadcast_to([P, 2, DH]),
                        rnv[:, t, HEADS:HEADS + 1], None, ALU.mult)
                ins.then_inc(aqk_n[s], 1)
                yield
                for quad in range(2):
                    for _ in range(4):
                        yield
                    dve.wait_ge(ao_ps[s], ao_ps.at(k, 4 * quad + 3))
                    o4 = [B4[:, 2 + t, 0:4 * (DH + 1)].rearrange("p (h d) -> p h d", h=4) for t in range(TILES)]
                    hs = slice(4 * quad, 4 * quad + 4)
                    link(*[dve.reciprocal(rsm[s][:, t, hs], o4[t][:, :, DH]) for t in range(TILES)])
                    for t in range(TILES):
                        ins = dve.tensor_tensor(
                            o[s][:, t, :].rearrange("p (h d) -> p h d", d=DH)[:, hs, :], o4[t][:, :, 0:DH],
                            rsm[s][:, t, hs].unsqueeze(2).broadcast_to([P, 4, DH]), ALU.mult)
                    ins.then_inc(ao_sb[s], 1)
                yield
                dve.wait_ge(proj_ps[s], proj_ps.at(k, 0))
                pr = B4[:, 2, 0:TOK].rearrange("p (t n) -> p t n", t=TILES)
                stats(lambda t: [pr[:, t, :]])
                yield from inverse_std(1)
                link(*[normed(z[s][:, t, :], pr[:, t, :], t) for t in range(TILES)])
                link(dve.tensor_tensor(z[s][:, :, :], z[s][:, :, :],
                                       outg[:, :].unsqueeze(1).broadcast_to([P, TILES, DIM]), ALU.mult))
                stats(lambda t: [z[s][:, t, :]])
                yield from inverse_std(2)
                link(*[normed(y[s][:, t, :], z[s][:, t, :], t) for t in range(TILES)])
                ins = dve.tensor_tensor(x1[s][:, :, :], xin[s][:, :, :], y[s][:, :, :], ALU.add)
                ins.then_inc(xfree[s], 1)
                dve.wait_ge(xfree[s], xfree.at(k, 0))
                stats(lambda t: [x1[s][:, t, :]])
                yield from inverse_std(3)
                for t in range(TILES):
                    ins = normed(h[s][:, t, :], x1[s][:, t, :], t)
                ins.then_inc(h_ready[s], 1)
                yield

                for l in range(DEPTH):
                    for t in range(TILES):
                        j = l * TILES + t
                        dve.wait_ge(qk_ps[s], qk_ps.at(k, j))
                        halves = [B4[:, part, :].rearrange("p (h a d) -> p h a d", a=2, d=DH // 2)
                                  for part in range(2)]
                        shape = [P, HEADS, 2, DH // 2]
                        if t:
                            dve.wait_ge(qk_rot[s], qk_rot.at(k, j - 1))
                        for part in range(2):
                            dve.wait_ge(qk_sq[s], qk_sq.at(k, 2 * j + part))
                            cs, sn = (tab[l][:, t, part, a, :].rearrange("p (a d) -> p a d", a=2)
                                      .unsqueeze(1).broadcast_to(shape) for a in range(2))
                            dst = [tt[s][:, part * INNER:(part + 1) * INNER]
                                   .rearrange("p (h a d) -> p h a d", a=2, d=DH // 2) for tt in (t1, t2)]
                            dve.tensor_tensor(dst[0], halves[part], cs, ALU.mult)
                            ins = dve.tensor_tensor(dst[1], halves[part][:, :, ::-1, :], sn, ALU.mult)
                        ins.then_inc(qk_t[s], 1)
                        link(dve.tensor_reduce(ss[s][:, t, :], sq[s][:, t, :].rearrange("p (h d) -> p h d", d=DH),
                                               AX_X, ALU.add))
                        dve.tensor_scalar(ss[s][:, t, :], ss[s][:, t, :], 1e-24, None, ALU.max).then_inc(ss_ready[s], 1)
                        dve.wait_ge(qk_t[s], qk_t.at(k, j))
                        dve.tensor_tensor(t1[s][:, :], t1[s][:, :], t2[s][:, :], ALU.add).then_inc(qk_rot[s], 1)
                        yield
                        dve.wait_ge(qk_rot[s], qk_rot.at(k, j))
                        dve.wait_ge(rn_ready[s], rn_ready.at(k, 1 + j))
                        dve.tensor_tensor(
                            qk[s][:, t, :].rearrange("p (h d) -> p h d", d=DH),
                            t1[s][:, :].rearrange("p (h d) -> p h d", d=DH),
                            rn[s][:, t, :].unsqueeze(2).broadcast_to([P, 2 * HEADS, DH]), ALU.mult).then_inc(qk_n[s], 1)
                        if t == 0:
                            dve.wait_ge(qk_n[s], qk_n.at(k, j))
                    yield

                    def negated_max(u):
                        dve.wait_ge(s_ps[s], s_ps.at(k, l * UNITS + u))
                        sc = B4[:, u % 2, :].rearrange("p (e n) -> p e n", e=2)[:, :, keys(u // PAIRS)]
                        dve.tensor_reduce(nmax[s][:, u, :], sc, AX_X, ALU.max, negate=True).then_inc(mx_ready[s], 1)

                    for u in range(UNITS):
                        t, _ = unit(u)
                        j = l * UNITS + u
                        negated_max(u)
                        yield
                        dve.wait_ge(pT_ps[s], pT_ps.at(k, j))
                        if u >= 2:
                            dve.wait_ge(pv_ps[s], pv_ps.at(k, j - 2))
                        nb = len(blocks(t))
                        dve.tensor_copy(
                            pT[s][u % 2][:, :, 0:nb, :],
                            B4[:, 2, 0:2 * nb * P].rearrange("p (e b n) -> p e b n", e=2, b=nb)).then_inc(pT_sb[s], 1)
                        yield
                        if u % PAIRS == PAIRS - 1:
                            dve.wait_ge(pv_ps[s], pv_ps.at(k, j))
                            link(dve.reciprocal(rsm[s][:, t, :], psm[s][:, t, :]))
                            dve.tensor_tensor(
                                o[s][:, t, :].rearrange("p (h d) -> p h d", d=DH),
                                B4[:, 3, :].rearrange("p (h d) -> p h d", d=DH),
                                rsm[s][:, t, :].unsqueeze(2).broadcast_to([P, HEADS, DH]), ALU.mult).then_inc(o_sb[s], 1)
                    yield
                    dve.wait_ge(proj_ps[s], proj_ps.at(k, 1 + l))
                    pr = B4[:, 2, 0:TOK].rearrange("p (t n) -> p t n", t=TILES)
                    dve.tensor_tensor(h[s][:, :, :], h[s][:, :, :], pr, ALU.add).then_inc(h_mid[s], 1)
                    yield
                    dve.wait_ge(sh_ps[s], sh_ps.at(k, l))
                    dve.wait_ge(h_mid[s], h_mid.at(k, l))
                    second = B4[:, 3, 0:TILES * 64].rearrange("p (t n) -> p t n", t=TILES)
                    stats(lambda t: [h[s][:, t, 0:64], second[:, t, :]])
                    yield from inverse_std(4 + l)
                    for t in range(TILES):
                        normed(y[s][:, t, 0:64], h[s][:, t, 0:64], t)
                        ins = normed(y[s][:, t, 64:128], second[:, t, :], t)
                    ins.then_inc(hn_ready[s], 1)
                    yield
                    for c, (_, n) in enumerate(HID_CHUNKS):
                        dve.wait_ge(gate_sb[s], gate_sb.at(k, l * NCH + c))
                        dve.scalar_tensor_tensor(
                            out=hid[s][0:n, c, :], in0=B4[0:n, 1 + c, 0:TOK], scalar=b1f[0:n, l, 0, c:c + 1],
                            in1=gate[s][0:n, c, :], op0=ALU.add, op1=ALU.mult).then_inc(hid_sb[s], 1)
                    yield
                    dve.wait_ge(f2_ps[s], f2_ps.at(k, l))
                    fo = B4[:, 0, 0:TOK].rearrange("p (t n) -> p t n", t=TILES)
                    dve.tensor_tensor(h[s][:, :, :], h[s][:, :, :], fo, ALU.add).then_inc(h_ready[s], 1)
                    yield
                dve.wait_ge(h_ready[s], h_ready.at(k, DEPTH))
                stats(lambda t: [h[s][:, t, :]])
                yield from inverse_std(4 + DEPTH)
                link(*[normed(y[s][:, t, :], h[s][:, t, :], t) for t in range(TILES)])
                dve.wait_ge(s_st[s], k * 16 + 16)
                dve.tensor_tensor(fin[s][:, :, :], x1[s][:, :, :], y[s][:, :, :], ALU.add).then_inc(fin_ready[s], 1)
                yield
                assert links[0] == LINKS, links[0]

            with dve.Fori(0, ROUNDS) as k:
                interleave([batch(s, k) for s in range(STREAMS)])

        @block.tensor
        def _(pe):
            pe.wait_ge(s_w, 16 * LOADS)
            for l in range(DEPTH):
                for part in range(2):
                    for c, (c0, n) in enumerate(HID_CHUNKS):
                        col = (l * 2 + part) * NCH + c
                        ins = pe.matmul(ps[0][0:n, 0, col:col + 1],
                                        w1_raw[l][:, part * HID + c0:part * HID + c0 + n], lnb[:, l:l + 1],
                                        start=True, stop=True)
            ins.then_inc(s_wp, 1)
            pe.wait_ge(s_wa, 2)
            pe.wait_ge(s_init, PRESETS)

            def batch(s, k):
                B4 = ps[s]

                def transpose4(dst, src):
                    for c in range(PAIRS):
                        ins = pe.transpose(dst[:, c * P:(c + 1) * P], src[:, c * P:(c + 1) * P], ident[:, :])
                    return ins

                pe.wait_ge(y_ready[s], y_ready.at(k, 0))
                for t in range(TILES):
                    ins = pe.transpose(B4[:, 3, t * P:(t + 1) * P], y[s][:, t, :], ident[:, :])
                ins.then_inc(act_ps[s], 1)
                yield
                pe.wait_ge(act_sb[s], act_sb.at(k, 0))
                for t in range(TILES):
                    pe.matmul(B4[:, t, :], actT[s][:, t * P:(t + 1) * P], wq_s[:, :],
                                         start=True, stop=True).then_inc(aq_ps[s], 1)
                for t in range(TILES):
                    ins = pe.matmul(B4[:, 2, t * P:(t + 1) * P], actT[s][:, t * P:(t + 1) * P], wkv_s[:, :],
                                    start=True, stop=True)
                ins.then_inc(aq_ps[s], 1)
                yield
                for t, bank in ((0, 3), (1, 0)):
                    pe.wait_ge(aqk_n[s], aqk_n.at(k, t))
                    transpose4(B4[:, bank, :], qk[s][:, t, 0:INNER]).then_inc(aqT_ps[s], 1)
                pe.wait_ge(aqk_n[s], aqk_n.at(k, 2))
                for t in range(TILES):
                    ins = pe.transpose(B4[:, 1, t * P:(t + 1) * P], qk[s][:, t, INNER:INNER + P], ident[:, :])
                ins.then_inc(aqT_ps[s], 1)
                yield
                pe.wait_ge(aqT_sb[s], aqT_sb.at(k, 2))
                pe.wait_ge(av_sb[s], av_sb.at(k, 0))

                def a_scores(hd):
                    if hd >= 2:
                        pe.wait_ge(ap_sb[s], ap_sb.at(k, hd - 2))
                    r = rows(hd % 2)
                    for kb in range(TILES):
                        ins = pe.matmul(B4[:, hd % 2, kb * TOK:(kb + 1) * TOK],
                                        kT[s][r, 0, kb * P:(kb + 1) * P], qT[s][r, hd // 2, :],
                                        start=True, stop=True)
                    ins.then_inc(as_ps[s], 1)

                def a_values(hd):
                    pe.wait_ge(ap_sb[s], ap_sb.at(k, hd))
                    if hd == 4:
                        pe.wait_ge(ao_sb[s], ao_sb.at(k, 0))
                    cols = slice((hd % 4) * (DH + 1), (hd % 4 + 1) * (DH + 1))
                    for t in range(TILES):
                        for kb in range(TILES):
                            ins = pe.matmul(B4[:, 2 + t, cols], pb[s][hd % 2][:, kb, t * P:(t + 1) * P],
                                            v1[s][:, kb, :], start=(kb == 0), stop=(kb == TILES - 1))
                    ins.then_inc(ao_ps[s], 1)

                a_scores(0)
                yield
                for hd in range(HEADS):
                    if hd + 1 < HEADS:
                        a_scores(hd + 1)
                    yield
                    a_values(hd)
                    yield

                def out_projection(n, w):
                    for t in range(TILES):
                        (pe.wait_ge(ao_sb[s], ao_sb.at(k, 1)) if n == 0 else
                         pe.wait_ge(o_sb[s], o_sb.at(k, (n - 1) * TILES + t)))
                        transpose4(B4[:, t, :], o[s][:, t, :]).then_inc(oT_ps[s], 1)
                    yield
                    for t in range(TILES):
                        pe.wait_ge(oT_sb[s], oT_sb.at(k, n * TILES + t))
                        for c in range(PAIRS):
                            ins = pe.matmul(B4[:, 2, t * P:(t + 1) * P], oT[s][:, c, t * P:(t + 1) * P],
                                            w[:, c, :], start=(c == 0), stop=(c == PAIRS - 1))
                    ins.then_inc(proj_ps[s], 1)
                    yield

                yield from out_projection(0, wout_s)
                for l in range(DEPTH):
                    pe.wait_ge(h_ready[s], h_ready.at(k, l))
                    for t in range(TILES):
                        ins = pe.transpose(B4[:, 3, t * P:(t + 1) * P], h[s][:, t, :], ident[:, :])
                    ins.then_inc(act_ps[s], 1)
                    yield
                    pe.wait_ge(act_sb[s], act_sb.at(k, 1 + 2 * l))

                    def project(t, part, bank):
                        return pe.matmul(B4[:, bank, :], shT[s][:, t * P:(t + 1) * P],
                                         wqkv_s[l][:, part * INNER:(part + 1) * INNER], start=True, stop=True)

                    def q_and_k(t):
                        project(t, 0, 0)
                        project(t, 1, 1).then_inc(qk_ps[s], 1)

                    q_and_k(0)
                    for t in range(TILES):
                        project(t, 2, 2 + t).then_inc(v_ps[s], 1)
                    yield
                    pe.wait_ge(qk_t[s], qk_t.at(k, l * TILES))
                    q_and_k(1)
                    yield
                    for t in range(TILES):
                        pe.wait_ge(qk_n[s], qk_n.at(k, l * TILES + t))
                        for part in range(2):
                            if t == 0:
                                pe.wait_ge(v_sb[s], v_sb.at(k, l * TILES + part))
                            dst = B4[:, (2 if t == 0 else 0) + part, :]
                            transpose4(dst, qk[s][:, t, part * INNER:(part + 1) * INNER]).then_inc(qkT_ps[s], 1)
                        yield
                    pe.wait_ge(qkT_sb[s], qkT_sb.at(k, (l + 1) * TILES * 2 - 1))

                    def scores(u):
                        t, heads = unit(u)
                        if u >= 2:
                            pe.wait_ge(p_sb[s], p_sb.at(k, l * UNITS + u - 2))
                        kk = keys(t)
                        sc = B4[:, u % 2, :].rearrange("p (e n) -> p e n", e=2)
                        pe.matmul(sc[:, :, kk], identb[:, :],
                                  maskb[:, t, kk].unsqueeze(1).broadcast_to([P, 2, kk.stop - kk.start]),
                                  start=True, stop=False)
                        for e, hd in enumerate(heads):
                            ins = pe.matmul(sc[:, e, kk], qT[s][rows(hd % 2), hd // 2, t * P:(t + 1) * P],
                                            kT[s][rows(hd % 2), hd // 2, kk], start=False, stop=(e == 1))
                        ins.then_inc(s_ps[s], 1)

                    def turn(u):
                        t, _ = unit(u)
                        j = l * UNITS + u
                        pe.wait_ge(p_sb[s], p_sb.at(k, j))
                        if u >= 1:
                            pe.wait_ge(pT_sb[s], pT_sb.at(k, j - 1))
                        nb = len(blocks(t))
                        for e in range(2):
                            for b in blocks(t):
                                ins = pe.transpose(B4[:, 2, (e * nb + b) * P:(e * nb + b + 1) * P],
                                                   pb[s][2 * t + u % 2][:, e, b * P:(b + 1) * P], ident[:, :])
                        ins.then_inc(pT_ps[s], 1)

                    def values(u):
                        t, heads = unit(u)
                        pe.wait_ge(pT_sb[s], pT_sb.at(k, l * UNITS + u))
                        if u == PAIRS:
                            pe.wait_ge(o_sb[s], o_sb.at(k, l * TILES))
                        for e, hd in enumerate(heads):
                            for b in blocks(t):
                                ins = pe.matmul(B4[:, 3, hd * DH:(hd + 1) * DH], pT[s][u % 2][:, e, b, :],
                                                v8[s][:, b, hd * DH:(hd + 1) * DH],
                                                start=(b == 0), stop=(b == t))
                        ins.then_inc(pv_ps[s], 1)

                    scores(0)
                    scores(1)
                    yield
                    for u in range(UNITS):
                        turn(u)
                        if u + 2 < UNITS:
                            scores(u + 2)
                        yield
                        values(u)
                        yield
                    yield from out_projection(1 + l, wo_s[l])
                    pe.wait_ge(h_mid[s], h_mid.at(k, l))
                    for t in range(TILES):
                        dst = B4[:, 3, t * 64:(t + 1) * 64]
                        ins = pe.matmul(dst, shift[:, 0, :], h[s][:, t, 64:128], start=True, stop=(t == 0))
                        if t:
                            ins = pe.matmul(dst, shift[:, 1, :], h[s][:, t - 1, 64:128], start=False, stop=True)
                    ins.then_inc(sh_ps[s], 1)
                    yield
                    pe.wait_ge(hn_ready[s], hn_ready.at(k, l))
                    for t in range(TILES):
                        ins = pe.transpose(B4[:, 0, t * P:(t + 1) * P], y[s][:, t, :], ident[:, :])
                    ins.then_inc(act_ps[s], 1)
                    yield
                    pe.wait_ge(act_sb[s], act_sb.at(k, 2 + 2 * l))
                    for c, (c0, n) in enumerate(HID_CHUNKS):
                        for part in range(2):
                            ins = pe.matmul(B4[0:n, 1 + c, part * TOK:(part + 1) * TOK],
                                            w1_s[l][:, part * HID + c0:part * HID + c0 + n],
                                            actT[s][:, 0:TOK], start=True, stop=True)
                        ins.then_inc(f1_ps[s], 1)
                    yield
                    for t in range(TILES):
                        for c, (_, n) in enumerate(HID_CHUNKS):
                            pe.wait_ge(hid_sb[s], hid_sb.at(k, l * NCH + c))
                            n += c == NCH - 1
                            ins = pe.matmul(B4[:, 0, t * P:(t + 1) * P], hid[s][0:n, c, t * P:(t + 1) * P],
                                            w2_s[l][0:n, c, :], start=(c == 0), stop=(c == NCH - 1))
                    ins.then_inc(f2_ps[s], 1)
                    yield

            with pe.Fori(0, ROUNDS) as k:
                interleave([batch(s, k) for s in range(STREAMS)])


def interleave(programs):
    while programs:
        programs = [p for p in programs if next(p, DONE) is not DONE]


_INS = ['L0_attn_x', 'L0_attn_norm_g', 'L0_attn_Wq', 'L0_attn_Wkv', 'L0_attn_Wout', 'L0_attn_out_norm_g',
        'L0_ffn_wqkv', 'L0_ffn_q_scale', 'L0_ffn_k_scale', 'L0_ffn_wo', 'L0_ffn_ln_g', 'L0_ffn_ln_b',
        'L0_ffn_w1', 'L0_ffn_b1', 'L0_ffn_w2', 'L0_ffn_b2']
_OUTS = [((16, 256, 128), 'float32')]


def kernel(**inputs):
    import numpy as _np
    import concourse.bacc as _bacc
    from concourse import mybir as _mybir
    from concourse.bass_utils import run_bass_kernel_spmd as _run

    nc = _bacc.Bacc("TRN2", target_bir_lowering=False, num_devices=1)
    given = {name: _np.ascontiguousarray(inputs[name]) for name in _INS}
    given.update(shape_constants())
    arrays, args = {}, []
    for name, a in given.items():
        arrays[f"in_{name}_dram"] = a
        args.append(nc.dram_tensor(f"in_{name}_dram", a.shape, _mybir.dt.from_np(a.dtype), kind="ExternalInput").ap())
    for i, (shape, dtype) in enumerate(_OUTS):
        dt = _mybir.dt.from_np(_np.dtype(dtype))
        args.append(nc.dram_tensor(f"out_{i}_dram", shape, dt, kind="ExternalOutput").ap())
    sandwich_kernel(nc, *args)
    r = _run(nc, [arrays], core_ids=[0])
    got = tuple(r.results[0][f"out_{i}_dram"] for i in range(len(_OUTS)))
    return got[0]
```

```python
from contextlib import ExitStack

import numpy as np

import concourse.bass as bass
from concourse import mybir
from concourse.alu_op_type import AluOpType as ALU

F32 = mybir.dt.float32
BF16 = mybir.dt.bfloat16
ACT = mybir.ActivationFunctionType
AX_X = mybir.AxisListType.X

P = 128
TOK = 256
TILES = TOK // P
DIM = 128
HEADS = 8
DH = 64
INNER = HEADS * DH
PAIRS = HEADS // 2
WINDOW = 64
DEPTH = 2
HID = int(DIM * 4 * 2 / 3)
HID_CHUNKS = [(c, min(P, HID - c)) for c in range(0, HID, P)]
NCH = len(HID_CHUNKS)
HID_LAST = HID_CHUNKS[-1][1]
EPS = 1e-5
QK_SCALE = 8.0
SIM_SCALE = 16.0
NEG = -1e30
STREAMS = 2
LOADS = 9 + DEPTH * (8 + 3 * NCH)
PRESETS = 3 + 7 * STREAMS
BLOCK_LINKS, ATTENTION_LINKS, FFN_LINKS, LAST_LINKS = 27, 4, 6, 6
UNITS = TILES * PAIRS
NORM_AT = 1
TURN_AT = 4



def shape_constants():
    half = np.arange(0, DH, 2, dtype=np.float32)
    inv_freq = (1.0 / np.float32(10000.0) ** (half / np.float32(DH))).astype(np.float32)
    t = np.arange(TOK, dtype=np.float32)
    freqs = t[:, None] * inv_freq[None, :]
    freqs = np.concatenate([freqs, freqs], axis=-1)
    base = (half + np.float32(0.4 * DH)) / np.float32(1.4 * DH)
    power = (t - TOK // 2) / np.float32(WINDOW // 2)
    scale = base[None, :] ** power[:, None]
    scale = np.concatenate([scale, scale], axis=-1)
    cos, sin = np.cos(freqs), np.sin(freqs)
    sign = np.where(np.arange(DH) < DH // 2, -1.0, 1.0).astype(np.float32)
    rot = np.stack([np.stack([cos * scale * QK_SCALE, sign * sin * scale * QK_SCALE], 1),
                    np.stack([cos / scale, sign * sin / scale], 1)], 1).astype(np.float32)
    rot = rot.reshape(TILES, P, 2, 2, DH).transpose(1, 0, 2, 3, 4)
    i, j = np.arange(TOK)[:, None], np.arange(TOK)[None, :]
    mask = np.where((i < j) | (i > j + WINDOW), NEG, 0.0).astype(np.float32)
    mask = mask.reshape(TILES, P, TOK).transpose(1, 0, 2)
    shift = np.zeros((P, 2, P), np.float32)
    shift[np.arange(P - 1), 0, np.arange(1, P)] = 1.0
    shift[P - 1, 1, 0] = 1.0
    return {
        "rot": np.ascontiguousarray(rot.reshape(P, -1)),
        "mask": np.ascontiguousarray(mask.reshape(P, -1)),
        "ident": np.eye(P, dtype=np.float32),
        "shift": shift.reshape(P, -1),
    }


def sandwich_kernel(nc: bass.Bass, x, norm_g, Wq, Wkv, Wout, out_norm_g, wqkv, q_scale, k_scale, wo,
                    ln_g, ln_b, w1, b1, w2, b2, rot_c, mask_c, ident_c, shift_c, out):
    B = x.shape[0]
    ROUNDS = B // STREAMS

    with ExitStack() as ctx:
        def sb(name, shape, dt=F32):
            return ctx.enter_context(nc.sbuf_tensor(name, shape, dt))

        def sem(name):
            return ctx.enter_context(nc.semaphore(name))

        def per_stream(make):
            return [make(s) for s in range(STREAMS)]

        ident = sb("ident", [P, P])
        identb = sb("identb", [P, P], BF16)
        shift = sb("shift", [P, 2, P])
        maskb = sb("maskb", [P, TILES, TOK], BF16)
        rot = sb("rot", [P, TILES, 2, 2, DH])
        qks = sb("qks", [P, DEPTH, 2, DH])
        tab = [sb(f"tab{l}", [P, TILES, 2, 2, DH]) for l in range(DEPTH)]
        ng = sb("ng", [P, 1])
        outg = sb("outg", [P, DIM])
        wq_s = sb("wq_s", [P, INNER])
        wkv_s = sb("wkv_s", [P, 2 * DH])
        wout_s = sb("wout_s", [P, PAIRS, DIM])
        wqkv_s = [sb(f"wqkv_s{l}", [P, 3 * INNER]) for l in range(DEPTH)]
        wo_s = [sb(f"wo_s{l}", [P, PAIRS, DIM]) for l in range(DEPTH)]
        w1_s = [sb(f"w1_s{l}", [P, 2 * HID]) for l in range(DEPTH)]
        w2_s = [sb(f"w2_s{l}", [P, NCH, DIM]) for l in range(DEPTH)]
        lng = sb("lng", [P, DEPTH])
        lnb = sb("lnb", [P, DEPTH])
        b1c = sb("b1c", [P, DEPTH, 2, NCH])
        b1f = sb("b1f", [P, DEPTH, 2, NCH])
        halfpow = sb("halfpow", [P, 2 * HEADS])
        floor = sb("floor", [P, HEADS + 1])

        xin = per_stream(lambda s: sb(f"xin{s}", [P, TILES, DIM]))
        x1 = per_stream(lambda s: sb(f"x1_{s}", [P, TILES, DIM]))
        y = per_stream(lambda s: sb(f"y{s}", [P, TILES, DIM]))
        z = per_stream(lambda s: sb(f"z{s}", [P, TILES, DIM]))
        h = per_stream(lambda s: sb(f"h{s}", [P, TILES, DIM]))
        fin = per_stream(lambda s: sb(f"fin{s}", [P, TILES, DIM]))
        st = per_stream(lambda s: sb(f"st{s}", [P, TILES, 2, 6]))
        aside = per_stream(lambda s: sb(f"aside{s}", [P, 1]))
        mv = per_stream(lambda s: sb(f"mv{s}", [P, TILES, 2]))
        arg = per_stream(lambda s: sb(f"arg{s}", [P, TILES]))
        rstd = per_stream(lambda s: sb(f"rstd{s}", [P, TILES]))
        actT = per_stream(lambda s: sb(f"actT{s}", [P, TOK + 1]))
        shT = per_stream(lambda s: sb(f"shT{s}", [P, TOK + 1]))
        sq = per_stream(lambda s: sb(f"sq{s}", [P, 2, 2 * INNER]))
        maskf = sq[1][:, 0, 0:TILES * TOK].rearrange("p (a n) -> p a n", a=TILES)
        w1_raw = [sq[0][:, l, 0:2 * HID] for l in range(DEPTH)]
        ss = per_stream(lambda s: sb(f"ss{s}", [P, TILES, 2 * HEADS]))
        rn = per_stream(lambda s: sb(f"rn{s}", [P, TILES, 2 * HEADS]))
        qk = per_stream(lambda s: sb(f"qk{s}", [P, TILES, 2 * INNER]))
        t1 = per_stream(lambda s: sb(f"t1_{s}", [P, TILES, 2 * INNER]))
        t2 = per_stream(lambda s: sb(f"t2_{s}", [P, TILES, 2 * INNER]))
        qT = per_stream(lambda s: sb(f"qT{s}", [P, PAIRS, TOK]))
        kT = per_stream(lambda s: sb(f"kT{s}", [P, 2, PAIRS, TOK]))
        v1 = per_stream(lambda s: sb(f"v1_{s}", [P, TILES, P]))
        v8 = per_stream(lambda s: sb(f"v8_{s}", [P, TILES, INNER]))
        pb = per_stream(lambda s: [sb(f"pb{s}_{b}", [P, 2, TOK]) for b in range(4)])
        pT = per_stream(lambda s: [sb(f"pT{s}_{b}", [P, 2, 2, P]) for b in range(2)])
        nmax = per_stream(lambda s: sb(f"nmax{s}", [P, UNITS, 2]))
        psm = per_stream(lambda s: sb(f"psm{s}", [P, TILES, HEADS]))
        rsm = per_stream(lambda s: sb(f"rsm{s}", [P, TILES, HEADS]))
        o = per_stream(lambda s: sb(f"o{s}", [P, TILES, INNER]))
        oT = per_stream(lambda s: sb(f"oT{s}", [P, PAIRS, TOK]))
        gate = per_stream(lambda s: sb(f"gate{s}", [P, NCH, TOK]))
        hid = per_stream(lambda s: sb(f"hid{s}", [P, NCH, TOK]))

        ps = per_stream(lambda s: ctx.enter_context(nc.psum_tensor(f"ps{s}", [P, 4, 512], F32)))

        s_w = sem("weights_loaded")
        s_wa = sem("weights_ready_dve")
        s_wp = sem("bias_product_ready")
        s_init = sem("presets_done")
        s_ld = [sem(f"x_loaded{s}") for s in range(STREAMS)]
        s_st = [sem(f"out_stored{s}") for s in range(STREAMS)]

        class Signal:

            def __init__(self, name, per):
                self.per = per
                self.sems = [sem(f"{name}{s}") for s in range(STREAMS)]

            def __getitem__(self, s):
                return self.sems[s]

            def at(self, k, n):
                return k * self.per + (n + 1)

        xfree = Signal("x_consumed", 1)
        own_block = Signal("dve_own_block", BLOCK_LINKS)
        own_attention = Signal("dve_own_attention", DEPTH * ATTENTION_LINKS)
        own_ffn = Signal("dve_own_ffn", DEPTH * FFN_LINKS)
        own_last = Signal("dve_own_last", LAST_LINKS)
        var_ready = Signal("variance_ready", 4 + DEPTH)
        rstd_ready = Signal("rstd_ready", 4 + DEPTH)
        y_ready = Signal("normed_ready", 1)
        act_ps = Signal("actT_in_psum", 1 + 2 * DEPTH)
        act_sb = Signal("actT_in_sbuf", 1 + 2 * DEPTH)
        aq_ps = Signal("a_qkv_in_psum", 3)
        aq_sq = Signal("a_squares_ready", 3)
        av_sb = Signal("a_v_ready", 1)
        ss_ready = Signal("norms_squared_ready", TILES * (1 + DEPTH))
        rn_ready = Signal("inverse_norms_ready", TILES * (1 + DEPTH))
        aqk_n = Signal("a_qk_normed", 3)
        aqT_ps = Signal("a_qkT_in_psum", 3)
        aqT_sb = Signal("a_qkT_in_sbuf", 3)
        as_ps = Signal("a_scores_in_psum", HEADS)
        ap_sb = Signal("a_probs_ready", HEADS)
        ao_ps = Signal("a_head_out_in_psum", HEADS)
        ao_sb = Signal("a_out_normed", 2)
        oT_ps = Signal("oT_in_psum", TILES * (1 + DEPTH))
        oT_sb = Signal("oT_in_sbuf", TILES * (1 + DEPTH))
        proj_ps = Signal("out_projection_in_psum", 1 + DEPTH)
        h_ready = Signal("residual_ready", 1 + DEPTH)
        h_mid = Signal("residual_after_attention", DEPTH)
        qk_ps = Signal("qk_in_psum", TILES * DEPTH)
        v_ps = Signal("v_in_psum", TILES * DEPTH)
        v_sb = Signal("v_in_sbuf", TILES * DEPTH)
        qk_sq = Signal("qk_squares_ready", 2 * TILES * DEPTH)
        qk_t = Signal("rotary_products_ready", TILES * DEPTH)
        qk_rot = Signal("rotary_sum_ready", TILES * DEPTH)
        qk_n = Signal("qk_rotated_normed", TILES * DEPTH)
        qkT_ps = Signal("qkT_in_psum", 2 * TILES * DEPTH)
        qkT_sb = Signal("qkT_in_sbuf", 2 * TILES * DEPTH)
        s_ps = Signal("scores_in_psum", UNITS * DEPTH)
        mx_ready = Signal("negated_max_ready", UNITS * DEPTH)
        p_sb = Signal("probs_ready", UNITS * DEPTH)
        pT_ps = Signal("probsT_in_psum", UNITS * DEPTH)
        pT_sb = Signal("probsT_in_sbuf", UNITS * DEPTH)
        pv_ps = Signal("head_out_in_psum", UNITS * DEPTH)
        o_sb = Signal("out_normed", TILES * DEPTH)
        sh_ps = Signal("shifted_half_in_psum", DEPTH)
        hn_ready = Signal("shifted_normed_ready", DEPTH)
        f1_ps = Signal("hidden_in_psum", NCH * DEPTH)
        gate_sb = Signal("gate_ready", NCH * DEPTH)
        hid_sb = Signal("hidden_ready", NCH * DEPTH)
        f2_ps = Signal("ffn_out_in_psum", DEPTH)
        fin_ready = Signal("result_ready", 1)

        def rows(n):
            return slice(64 * n, 64 * n + 64)

        def keys(t):
            return slice(max(t * P - WINDOW, 0), (t + 1) * P)

        def unit(u):
            t, n = divmod(u, PAIRS)
            return t, [4 * (n // 2) + n % 2, 4 * (n // 2) + 2 + n % 2]

        def blocks(t):
            return range(t + 1)

        x_v = x.rearrange("b (t p) d -> b p t d", p=P)
        out_v = out.rearrange("b (t p) d -> b p t d", p=P)

        block = ctx.enter_context(nc.Block())

        @block.sync
        def _(sp):
            loads = [0]

            def load(dst, src):
                sp.dma_start(dst, src).then_inc(s_w, 16)
                loads[0] += 1

            for s in range(STREAMS):
                sp.dma_start(xin[s][:, :, :], x_v[s]).then_inc(s_ld[s], 16)
                sp.sem_inc(s_st[s], 16)
            load(ident[:, :], ident_c)
            load(ng[:, :], norm_g.rearrange("(p a) -> p a", a=1))
            load(wq_s[:, :], Wq)
            load(wkv_s[:, :], Wkv)
            load(wout_s[:, :, :], Wout.rearrange("(c p) n -> p c n", p=P))
            load(outg[:, :], out_norm_g.partition_broadcast(P))
            load(shift[:, :, :], shift_c.rearrange("p (a n) -> p a n", a=2))
            load(maskf[:, :, :], mask_c.rearrange("p (a n) -> p a n", a=TILES))
            load(rot[:, :, :, :, :], rot_c.rearrange("p (t a b d) -> p t a b d", t=TILES, a=2, b=2))
            for l in range(DEPTH):
                load(wqkv_s[l][:, :], wqkv[l])
                load(qks[:, l, 0, :], q_scale[l].partition_broadcast(P))
                load(qks[:, l, 1, :], k_scale[l].partition_broadcast(P))
                load(wo_s[l][:, :, :], wo[l].rearrange("(c p) n -> p c n", p=P))
                load(lng[:, l:l + 1], ln_g[l].rearrange("(p a) -> p a", a=1))
                load(lnb[:, l:l + 1], ln_b[l].rearrange("(p a) -> p a", a=1))
                load(w1_raw[l][:, :], w1[l])
                for c, (c0, n) in enumerate(HID_CHUNKS):
                    for part in range(2):
                        load(b1c[0:n, l, part, c:c + 1],
                             b1[l, part * HID + c0:part * HID + c0 + n].rearrange("(p a) -> p a", a=1))
                    load(w2_s[l][0:n, c, :], w2[l, c0:c0 + n, :])
                load(w2_s[l][HID_LAST:HID_LAST + 1, NCH - 1, :], b2[l:l + 1, :])
            assert loads[0] == LOADS, loads[0]

            def store(s, k, b):
                sp.wait_ge(fin_ready[s], fin_ready.at(k, 0))
                sp.dma_start(out_v[b], fin[s][:, :, :]).then_inc(s_st[s], 16)

            with sp.Fori(0, ROUNDS - 1) as k:
                for s in range(STREAMS):
                    sp.wait_ge(xfree[s], xfree.at(k, 0))
                    sp.dma_start(xin[s][:, :, :], x_v[(k + 1) * STREAMS + s]).then_inc(s_ld[s], 16)
                for s in range(STREAMS):
                    store(s, k, k * STREAMS + s)
            for s in range(STREAMS):
                store(s, ROUNDS - 1, (ROUNDS - 1) * STREAMS + s)
            for s in range(STREAMS):
                sp.wait_ge(s_st[s], 16 * (ROUNDS + 1))

        @block.gpsimd
        def _(pool):
            pool.memset(halfpow[:, :], -0.5).then_inc(s_init, 1)
            pool.memset(floor[:, 0:HEADS], (1e-12 / SIM_SCALE) ** 2).then_inc(s_init, 1)
            pool.memset(floor[:, HEADS:HEADS + 1], 1e-24).then_inc(s_init, 1)
            for s in range(STREAMS):
                pool.memset(v1[s][:, :, DH:DH + 1], 1.0).then_inc(s_init, 1)
                pool.memset(v1[s][:, :, DH + 1:P], 0.0).then_inc(s_init, 1)
                pool.memset(kT[s][:, :, :, :], 0.0).then_inc(s_init, 1)
                pool.memset(shT[s][:, :], 0.0).then_inc(s_init, 1)
                pool.memset(hid[s][:, :, :], 1.0).then_inc(s_init, 1)
                for b in range(2, 4):
                    pool.memset(pb[s][b][:, :, 0:WINDOW], 0.0).then_inc(s_init, 1)
            pool.wait_ge(s_init, PRESETS)

            def parts(s, k):
                def norm_rstd(n):
                    pool.wait_ge(var_ready[s], var_ready.at(k, n))
                    pool.tensor_tensor(rstd[s][:, :], arg[s][:, :], halfpow[:, 0:TILES],
                                       ALU.pow).then_inc(rstd_ready[s], 1)

                def attention_block():
                    yield
                    norm_rstd(0)
                    for t in range(TILES):
                        yield
                        pool.wait_ge(ss_ready[s], ss_ready.at(k, t))
                        pool.tensor_tensor(rn[s][:, t, 0:HEADS + 1], ss[s][:, t, 0:HEADS + 1],
                                           halfpow[:, 0:HEADS + 1], ALU.pow).then_inc(rn_ready[s], 1)
                    for n in range(2):
                        yield
                        norm_rstd(1 + n)

                def layer_attention(l):
                    for t in range(TILES):
                        j = l * TILES + t
                        yield
                        pool.wait_ge(ss_ready[s], ss_ready.at(k, TILES + j))
                        pool.tensor_tensor(rn[s][:, t, :], ss[s][:, t, :], halfpow[:, 0:2 * HEADS],
                                           ALU.pow).then_inc(rn_ready[s], 1)

                def layer_ffn(l):
                    yield
                    norm_rstd(3 + l)

                def last_norm():
                    yield
                    norm_rstd(3 + DEPTH)

                return attention_block, layer_attention, layer_ffn, last_norm

            with pool.Fori(0, ROUNDS) as k:
                interleave(TURNS["gpsimd"], [whole_batch(*parts(s, k)) for s in range(STREAMS)])

        @block.scalar
        def _(act):
            act.wait_ge(s_init, PRESETS)
            act.wait_ge(s_wa, 2)
            copy, square = ACT.Copy, ACT.Square

            def parts(s, k):
                B4 = ps[s]

                def out_T(n):
                    for t in range(TILES):
                        yield
                        act.wait_ge(oT_ps[s], oT_ps.at(k, n * TILES + t))
                        act.activation(oT[s][:, :, t * P:(t + 1) * P],
                                       B4[:, t, :].rearrange("p (c n) -> p c n", c=PAIRS),
                                       copy).then_inc(oT_sb[s], 1)

                def attention_block():
                    yield
                    act.wait_ge(act_ps[s], act_ps.at(k, 0))
                    act.activation(actT[s][:, 0:TOK], B4[:, 3, 0:TOK], copy).then_inc(act_sb[s], 1)
                    yield
                    act.wait_ge(aq_ps[s], aq_ps.at(k, 0))
                    kv = B4[:, 2, 0:TILES * 2 * DH].rearrange("p (t n) -> p t n", t=TILES)
                    act.activation(sq[s][:, :, INNER:INNER + DH], kv[:, :, 0:DH], square).then_inc(aq_sq[s], 1)
                    act.activation(v1[s][:, :, 0:DH], kv[:, :, DH:2 * DH], copy).then_inc(av_sb[s], 1)
                    for t in range(TILES):
                        yield
                        act.wait_ge(aq_ps[s], aq_ps.at(k, 1 + t))
                        act.activation(sq[s][:, t, 0:INNER], B4[:, t, :], square).then_inc(aq_sq[s], 1)
                    for t, bank in ((0, 3), (1, 0)):
                        yield
                        act.wait_ge(aqT_ps[s], aqT_ps.at(k, t))
                        act.activation(qT[s][:, :, t * P:(t + 1) * P],
                                       B4[:, bank, :].rearrange("p (c n) -> p c n", c=PAIRS),
                                       copy).then_inc(aqT_sb[s], 1)
                    yield
                    act.wait_ge(aqT_ps[s], aqT_ps.at(k, 2))
                    for e in range(2):
                        ins = act.activation(kT[s][rows(e), e, 0, :], B4[rows(e), 1, 0:TOK], copy)
                    ins.then_inc(aqT_sb[s], 1)
                    for hd in range(HEADS):
                        yield
                        act.wait_ge(as_ps[s], as_ps.at(k, hd))
                        if hd >= 2:
                            act.wait_ge(ao_ps[s], ao_ps.at(k, hd - 2))
                        act.activation(pb[s][hd % 2][:, :, :].rearrange("p a n -> p (a n)"),
                                       B4[:, hd % 2, :], ACT.Exp, scale=SIM_SCALE).then_inc(ap_sb[s], 1)
                    yield from out_T(0)

                def layer_attention(l):
                    yield
                    act.wait_ge(act_ps[s], act_ps.at(k, 1 + 2 * l))
                    act.activation(shT[s][0:64, 0:TOK], B4[0:64, 3, 0:TOK], copy)
                    act.activation(shT[s][64:128, 1:TOK + 1], B4[64:128, 3, 0:TOK], copy).then_inc(act_sb[s], 1)
                    for t in range(TILES):
                        j = l * TILES + t
                        yield
                        act.wait_ge(qk_ps[s], qk_ps.at(k, j))
                        for part in range(2):
                            act.activation(sq[s][:, t, part * INNER:(part + 1) * INNER], B4[:, part, :],
                                           square).then_inc(qk_sq[s], 1)
                        yield
                        act.wait_ge(v_ps[s], v_ps.at(k, j))
                        act.activation(v8[s][:, t, :], B4[:, 2 + t, :], copy).then_inc(v_sb[s], 1)
                    def turned(t, bank):
                        q_ps, k_ps = (B4[:, bank + part, :].rearrange("p (c n) -> p c n", c=PAIRS)
                                      for part in range(2))
                        yield
                        act.wait_ge(qkT_ps[s], qkT_ps.at(k, (l * TILES + t) * 2))
                        act.activation(qT[s][:, :, t * P:(t + 1) * P], q_ps, copy).then_inc(qkT_sb[s], 1)
                        yield
                        act.wait_ge(qkT_ps[s], qkT_ps.at(k, (l * TILES + t) * 2 + 1))
                        for e in range(2):
                            ins = act.activation(kT[s][rows(e), e, :, t * P:(t + 1) * P], k_ps[rows(e)], copy)
                        ins.then_inc(qkT_sb[s], 1)

                    yield from turned(0, 2)
                    for u in range(UNITS):
                        t, heads = unit(u)
                        j = l * UNITS + u
                        if u == TURN_AT:
                            yield from turned(1, 0)
                        yield
                        act.wait_ge(mx_ready[s], mx_ready.at(k, j))
                        if u >= 2:
                            act.wait_ge(pT_ps[s], pT_ps.at(k, j - 2))
                        for e, hd in enumerate(heads):
                            ins = act.activation(pb[s][2 * t + u % 2][:, e, keys(t)],
                                                 B4[:, u % 2, :].rearrange("p (e n) -> p e n", e=2)[:, e, keys(t)],
                                                 ACT.Exp, bias=nmax[s][:, u, e:e + 1],
                                                 accum_out=psm[s][:, t, hd:hd + 1])
                        ins.then_inc(p_sb[s], 1)
                    yield from out_T(1 + l)

                def layer_ffn(l):
                    yield
                    act.wait_ge(act_ps[s], act_ps.at(k, 2 + 2 * l))
                    act.activation(actT[s][:, 0:TOK], B4[:, 0, 0:TOK], copy).then_inc(act_sb[s], 1)
                    for c, (_, n) in enumerate(HID_CHUNKS):
                        yield
                        act.wait_ge(f1_ps[s], f1_ps.at(k, l * NCH + c))
                        act.activation(gate[s][0:n, c, :], B4[0:n, 1 + c, TOK:2 * TOK], ACT.Gelu,
                                       bias=b1f[0:n, l, 1, c:c + 1]).then_inc(gate_sb[s], 1)

                return attention_block, layer_attention, layer_ffn, nothing

            with act.Fori(0, ROUNDS) as k:
                interleave(TURNS["scalar"], [whole_batch(*parts(s, k)) for s in range(STREAMS)])

        @block.vector
        def _(dve):
            dve.wait_ge(s_w, 16 * LOADS)
            dve.tensor_scalar(wq_s[:, :], wq_s[:, :], ng[:, 0:1], None, ALU.mult)
            dve.tensor_scalar(wkv_s[:, :], wkv_s[:, :], ng[:, 0:1], None, ALU.mult)
            dve.tensor_copy(identb[:, :], ident[:, :])
            dve.tensor_copy(maskb[:, :, :], maskf[:, :, :])
            for l in range(DEPTH):
                dve.tensor_scalar(w1_s[l][:, :], w1_raw[l][:, :], lng[:, l:l + 1], None, ALU.mult)
                for t in range(TILES):
                    for part in range(2):
                        qs = qks[:, l, part, :]
                        dve.tensor_tensor(tab[l][:, t, part, 0, :], rot[:, t, part, 0, :], qs, ALU.mult)
                        ins = dve.tensor_tensor(
                            tab[l][:, t, part, 1, :].rearrange("p (a d) -> p a d", a=2),
                            rot[:, t, part, 1, :].rearrange("p (a d) -> p a d", a=2),
                            qs.rearrange("p (a d) -> p a d", a=2)[:, ::-1, :], ALU.mult)
            ins.then_inc(s_wa, 1)
            dve.wait_ge(s_wp, 1)
            for l in range(DEPTH):
                for part in range(2):
                    for c, (_, n) in enumerate(HID_CHUNKS):
                        col = (l * 2 + part) * NCH + c
                        ins = dve.tensor_tensor(b1f[0:n, l, part, c:c + 1], b1c[0:n, l, part, c:c + 1],
                                                ps[0][0:n, 0, col:col + 1], ALU.add)
            ins.then_inc(s_wa, 1)
            dve.wait_ge(s_init, PRESETS)

            def parts(s, k):
                B4 = ps[s]
                chain = []

                def link(*instructions):
                    own = chain[0]
                    for ins in instructions:
                        ins.then_inc(own[s], 1)
                        chain[1] += 1
                    dve.wait_ge(own[s], own.at(k, chain[1] - 1))

                def stats(pieces):
                    link(*[dve.bn_stats(st[s][:, t, a, :], piece)
                           for t in range(TILES) for a, piece in enumerate(pieces(t))])
                    dve.memset(aside[s][:, :], 0.0)
                    link(*[dve.bn_aggr(mv[s][:, t, :], st[s][:, t, 0:len(pieces(t)), :])
                           for t in range(TILES)])

                def variance(times=1.0, plus=EPS):
                    dve.tensor_scalar(arg[s][:, :], mv[s][:, :, 1], times, plus,
                                      ALU.mult, ALU.add).then_inc(var_ready[s], 1)

                def normed(dst, src, t):
                    return dve.tensor_scalar(dst, src, mv[s][:, t, 0:1], rstd[s][:, t:t + 1],
                                             ALU.subtract, ALU.mult)

                def attention_block():
                    yield
                    chain[:] = own_block, 0
                    dve.wait_ge(s_ld[s], k * 16 + 16)
                    stats(lambda t: [xin[s][:, t, :]])
                    variance(1.0 + EPS, EPS * EPS)
                    yield
                    dve.wait_ge(rstd_ready[s], rstd_ready.at(k, 0))
                    for t in range(TILES):
                        ins = normed(y[s][:, t, :], xin[s][:, t, :], t)
                    ins.then_inc(y_ready[s], 1)
                    for t in range(TILES):
                        yield
                        dve.wait_ge(aq_sq[s], aq_sq.at(k, 1 + t))
                        link(dve.tensor_reduce(ss[s][:, t, 0:HEADS + 1], sq[s][:, t, 0:INNER + DH]
                                               .rearrange("p (h d) -> p h d", d=DH), AX_X, ALU.add))
                        dve.tensor_tensor(ss[s][:, t, 0:HEADS + 1], ss[s][:, t, 0:HEADS + 1], floor[:, :],
                                          ALU.max).then_inc(ss_ready[s], 1)
                    for t in range(TILES):
                        yield
                        dve.wait_ge(rn_ready[s], rn_ready.at(k, t))
                        dve.tensor_tensor(
                            qk[s][:, t, 0:INNER].rearrange("p (h d) -> p h d", d=DH),
                            B4[:, t, :].rearrange("p (h d) -> p h d", d=DH),
                            rn[s][:, t, 0:HEADS].unsqueeze(2).broadcast_to([P, HEADS, DH]),
                            ALU.mult).then_inc(aqk_n[s], 1)
                    yield
                    dve.wait_ge(av_sb[s], av_sb.at(k, 0))
                    for t in range(TILES):
                        ins = dve.tensor_scalar(
                            qk[s][:, t, INNER:INNER + P].rearrange("p (a d) -> p a d", a=2),
                            B4[:, 2, t * 2 * DH:t * 2 * DH + DH].unsqueeze(1).broadcast_to([P, 2, DH]),
                            rn[s][:, t, HEADS:HEADS + 1], None, ALU.mult)
                    ins.then_inc(aqk_n[s], 1)
                    for quad in range(2):
                        yield
                        dve.wait_ge(ao_ps[s], ao_ps.at(k, 4 * quad + 3))
                        o4 = [B4[:, 2 + t, :].rearrange("p (h d) -> p h d", h=4) for t in range(TILES)]
                        hs = slice(4 * quad, 4 * quad + 4)
                        link(*[dve.reciprocal(rsm[s][:, t, hs], o4[t][:, :, DH]) for t in range(TILES)])
                        for t in range(TILES):
                            ins = dve.tensor_tensor(
                                o[s][:, t, :].rearrange("p (h d) -> p h d", d=DH)[:, hs, :], o4[t][:, :, 0:DH],
                                rsm[s][:, t, hs].unsqueeze(2).broadcast_to([P, 4, DH]), ALU.mult)
                        ins.then_inc(ao_sb[s], 1)
                    yield
                    dve.wait_ge(proj_ps[s], proj_ps.at(k, 0))
                    pr = B4[:, 2, 0:TOK].rearrange("p (t n) -> p t n", t=TILES)
                    stats(lambda t: [pr[:, t, :]])
                    link(dve.tensor_scalar(arg[s][:, :], mv[s][:, :, 1], EPS, EPS, ALU.add, ALU.mult),
                         *[dve.scalar_tensor_tensor(out=z[s][:, t, :], in0=pr[:, t, :], scalar=mv[s][:, t, 0:1],
                                                    in1=outg[:, :], op0=ALU.subtract, op1=ALU.mult)
                           for t in range(TILES)])
                    stats(lambda t: [z[s][:, t, :]])
                    dve.tensor_tensor(arg[s][:, :], arg[s][:, :], mv[s][:, :, 1], ALU.add).then_inc(var_ready[s], 1)
                    yield
                    dve.wait_ge(rstd_ready[s], rstd_ready.at(k, 1))
                    link(*[normed(y[s][:, t, :], z[s][:, t, :], t) for t in range(TILES)])
                    dve.tensor_tensor(x1[s][:, :, :], xin[s][:, :, :], y[s][:, :, :],
                                      ALU.add).then_inc(xfree[s], 1)
                    dve.wait_ge(xfree[s], xfree.at(k, 0))
                    stats(lambda t: [x1[s][:, t, :]])
                    variance()
                    yield
                    dve.wait_ge(rstd_ready[s], rstd_ready.at(k, 2))
                    for t in range(TILES):
                        ins = normed(h[s][:, t, :], x1[s][:, t, :], t)
                    ins.then_inc(h_ready[s], 1)

                def layer_attention(l):
                    def normed_qk(t):
                        j = l * TILES + t
                        dve.wait_ge(qk_rot[s], qk_rot.at(k, j))
                        dve.wait_ge(rn_ready[s], rn_ready.at(k, TILES + j))
                        dve.tensor_tensor(
                            qk[s][:, t, :].rearrange("p (h d) -> p h d", d=DH),
                            t1[s][:, t, :].rearrange("p (h d) -> p h d", d=DH),
                            rn[s][:, t, :].unsqueeze(2).broadcast_to([P, 2 * HEADS, DH]),
                            ALU.mult).then_inc(qk_n[s], 1)

                    def rotary_products(t):
                        j = l * TILES + t
                        dve.wait_ge(qk_ps[s], qk_ps.at(k, j))
                        shape = [P, HEADS, 2, DH // 2]
                        for part in range(2):
                            half = B4[:, part, :].rearrange("p (h a d) -> p h a d", a=2, d=DH // 2)
                            cs, sn = (tab[l][:, t, part, a, :].rearrange("p (a d) -> p a d", a=2)
                                      .unsqueeze(1).broadcast_to(shape) for a in range(2))
                            dst = [tt[s][:, t, part * INNER:(part + 1) * INNER]
                                   .rearrange("p (h a d) -> p h a d", a=2, d=DH // 2) for tt in (t1, t2)]
                            dve.wait_ge(qk_sq[s], qk_sq.at(k, 2 * j + part))
                            dve.tensor_tensor(dst[0], half, cs, ALU.mult)
                            ins = dve.tensor_tensor(dst[1], half[:, :, ::-1, :], sn, ALU.mult)
                        ins.then_inc(qk_t[s], 1)

                    def squared_norms(t):
                        link(dve.tensor_reduce(ss[s][:, t, :], sq[s][:, t, :].rearrange("p (h d) -> p h d", d=DH),
                                               AX_X, ALU.add))
                        dve.tensor_scalar(ss[s][:, t, :], ss[s][:, t, :], 1e-24, None,
                                          ALU.max).then_inc(ss_ready[s], 1)

                    def rotary_sum(t):
                        dve.wait_ge(qk_t[s], qk_t.at(k, l * TILES + t))
                        dve.tensor_tensor(t1[s][:, t, :], t1[s][:, t, :], t2[s][:, t, :],
                                          ALU.add).then_inc(qk_rot[s], 1)

                    yield
                    chain[:] = own_attention, l * ATTENTION_LINKS
                    rotary_products(0)
                    yield
                    squared_norms(0)
                    yield
                    rotary_sum(0)
                    yield
                    rotary_products(1)
                    yield
                    normed_qk(0)
                    yield
                    squared_norms(1)
                    yield
                    rotary_sum(1)

                    def negated_max(u):
                        dve.wait_ge(s_ps[s], s_ps.at(k, l * UNITS + u))
                        sc = B4[:, u % 2, :].rearrange("p (e n) -> p e n", e=2)[:, :, keys(unit(u)[0])]
                        dve.tensor_reduce(nmax[s][:, u, :], sc, AX_X, ALU.max, negate=True).then_inc(mx_ready[s], 1)

                    yield
                    negated_max(0)
                    for u in range(UNITS):
                        t, _ = unit(u)
                        j = l * UNITS + u
                        if u + 1 < UNITS:
                            yield
                            negated_max(u + 1)
                        if u == NORM_AT:
                            yield
                            normed_qk(1)
                        yield
                        dve.wait_ge(pT_ps[s], pT_ps.at(k, j))
                        if u >= 2:
                            dve.wait_ge(pv_ps[s], pv_ps.at(k, j - 2))
                        nb = len(blocks(t))
                        dve.tensor_copy(
                            pT[s][u % 2][:, :, 0:nb, :],
                            B4[:, 2, 0:2 * nb * P].rearrange("p (e b n) -> p e b n", e=2, b=nb)
                        ).then_inc(pT_sb[s], 1)
                        if u % PAIRS == PAIRS - 1:
                            yield
                            dve.wait_ge(pv_ps[s], pv_ps.at(k, j))
                            link(dve.reciprocal(rsm[s][:, t, :], psm[s][:, t, :]))
                            dve.tensor_tensor(
                                o[s][:, t, :].rearrange("p (h d) -> p h d", d=DH),
                                B4[:, 3, :].rearrange("p (h d) -> p h d", d=DH),
                                rsm[s][:, t, :].unsqueeze(2).broadcast_to([P, HEADS, DH]),
                                ALU.mult).then_inc(o_sb[s], 1)
                    yield
                    dve.wait_ge(proj_ps[s], proj_ps.at(k, 1 + l))
                    pr = B4[:, 2, 0:TOK].rearrange("p (t n) -> p t n", t=TILES)
                    dve.tensor_tensor(h[s][:, :, :], h[s][:, :, :], pr, ALU.add).then_inc(h_mid[s], 1)

                def layer_ffn(l):
                    yield
                    chain[:] = own_ffn, l * FFN_LINKS
                    dve.wait_ge(sh_ps[s], sh_ps.at(k, l))
                    dve.wait_ge(h_mid[s], h_mid.at(k, l))
                    second = B4[:, 3, 0:TILES * 64].rearrange("p (t n) -> p t n", t=TILES)
                    stats(lambda t: [h[s][:, t, 0:64], second[:, t, :]])
                    variance()
                    yield
                    dve.wait_ge(rstd_ready[s], rstd_ready.at(k, 3 + l))
                    for t in range(TILES):
                        normed(y[s][:, t, 0:64], h[s][:, t, 0:64], t)
                        ins = normed(y[s][:, t, 64:128], second[:, t, :], t)
                    ins.then_inc(hn_ready[s], 1)
                    for c, (_, n) in enumerate(HID_CHUNKS):
                        yield
                        dve.wait_ge(gate_sb[s], gate_sb.at(k, l * NCH + c))
                        dve.scalar_tensor_tensor(
                            out=hid[s][0:n, c, :], in0=B4[0:n, 1 + c, 0:TOK], scalar=b1f[0:n, l, 0, c:c + 1],
                            in1=gate[s][0:n, c, :], op0=ALU.add, op1=ALU.mult).then_inc(hid_sb[s], 1)
                    yield
                    dve.wait_ge(f2_ps[s], f2_ps.at(k, l))
                    fo = B4[:, 0, 0:TOK].rearrange("p (t n) -> p t n", t=TILES)
                    dve.tensor_tensor(h[s][:, :, :], h[s][:, :, :], fo, ALU.add).then_inc(h_ready[s], 1)

                def last_norm():
                    yield
                    chain[:] = own_last, 0
                    dve.wait_ge(h_ready[s], h_ready.at(k, DEPTH))
                    stats(lambda t: [h[s][:, t, :]])
                    variance()
                    yield
                    dve.wait_ge(rstd_ready[s], rstd_ready.at(k, 3 + DEPTH))
                    link(*[normed(y[s][:, t, :], h[s][:, t, :], t) for t in range(TILES)])
                    yield
                    dve.wait_ge(s_st[s], k * 16 + 16)
                    dve.tensor_tensor(fin[s][:, :, :], x1[s][:, :, :], y[s][:, :, :],
                                      ALU.add).then_inc(fin_ready[s], 1)
                    assert chain[1] == LAST_LINKS, chain[1]

                return attention_block, layer_attention, layer_ffn, last_norm

            with dve.Fori(0, ROUNDS) as k:
                interleave(TURNS["vector"], [whole_batch(*parts(s, k)) for s in range(STREAMS)])

        @block.tensor
        def _(pe):
            pe.wait_ge(s_w, 16 * LOADS)
            for l in range(DEPTH):
                for part in range(2):
                    for c, (c0, n) in enumerate(HID_CHUNKS):
                        col = (l * 2 + part) * NCH + c
                        ins = pe.matmul(ps[0][0:n, 0, col:col + 1],
                                        w1_raw[l][:, part * HID + c0:part * HID + c0 + n], lnb[:, l:l + 1],
                                        start=True, stop=True)
            ins.then_inc(s_wp, 1)
            pe.wait_ge(s_wa, 2)
            pe.wait_ge(s_init, PRESETS)

            def parts(s, k):
                B4 = ps[s]

                def transpose4(dst, src):
                    for c in range(PAIRS):
                        ins = pe.transpose(dst[:, c * P:(c + 1) * P], src[:, c * P:(c + 1) * P], ident[:, :])
                    return ins

                def out_projection(n, w):
                    for t in range(TILES):
                        yield
                        if n == 0:
                            pe.wait_ge(ao_sb[s], ao_sb.at(k, 1))
                        else:
                            pe.wait_ge(o_sb[s], o_sb.at(k, (n - 1) * TILES + t))
                        transpose4(B4[:, t, :], o[s][:, t, :]).then_inc(oT_ps[s], 1)
                    for t in range(TILES):
                        yield
                        pe.wait_ge(oT_sb[s], oT_sb.at(k, n * TILES + t))
                        for c in range(PAIRS):
                            ins = pe.matmul(B4[:, 2, t * P:(t + 1) * P], oT[s][:, c, t * P:(t + 1) * P],
                                            w[:, c, :], start=(c == 0), stop=(c == PAIRS - 1))
                    ins.then_inc(proj_ps[s], 1)

                def attention_block():
                    yield
                    pe.wait_ge(y_ready[s], y_ready.at(k, 0))
                    for t in range(TILES):
                        ins = pe.transpose(B4[:, 3, t * P:(t + 1) * P], y[s][:, t, :], ident[:, :])
                    ins.then_inc(act_ps[s], 1)
                    yield
                    pe.wait_ge(act_sb[s], act_sb.at(k, 0))
                    for t in range(TILES):
                        ins = pe.matmul(B4[:, 2, t * P:(t + 1) * P], actT[s][:, t * P:(t + 1) * P], wkv_s[:, :],
                                        start=True, stop=True)
                    ins.then_inc(aq_ps[s], 1)
                    for t in range(TILES):
                        pe.matmul(B4[:, t, :], actT[s][:, t * P:(t + 1) * P], wq_s[:, :],
                                  start=True, stop=True).then_inc(aq_ps[s], 1)
                    for t, bank in ((0, 3), (1, 0)):
                        yield
                        pe.wait_ge(aqk_n[s], aqk_n.at(k, t))
                        transpose4(B4[:, bank, :], qk[s][:, t, 0:INNER]).then_inc(aqT_ps[s], 1)
                    yield
                    pe.wait_ge(aqk_n[s], aqk_n.at(k, 2))
                    for t in range(TILES):
                        ins = pe.transpose(B4[:, 1, t * P:(t + 1) * P], qk[s][:, t, INNER:INNER + P], ident[:, :])
                    ins.then_inc(aqT_ps[s], 1)

                    def scores(hd):
                        if hd >= 2:
                            pe.wait_ge(ap_sb[s], ap_sb.at(k, hd - 2))
                        for kb in range(TILES):
                            ins = pe.matmul(B4[:, hd % 2, kb * TOK:(kb + 1) * TOK],
                                            kT[s][:, hd % 2, 0, kb * P:(kb + 1) * P], qT[s][:, hd // 2, :],
                                            start=True, stop=True)
                        ins.then_inc(as_ps[s], 1)

                    def values(hd):
                        pe.wait_ge(ap_sb[s], ap_sb.at(k, hd))
                        if hd == 4:
                            pe.wait_ge(ao_sb[s], ao_sb.at(k, 0))
                        cols = slice((hd % 4) * P, (hd % 4 + 1) * P)
                        for t in range(TILES):
                            for kb in range(TILES):
                                ins = pe.matmul(B4[:, 2 + t, cols], pb[s][hd % 2][:, kb, t * P:(t + 1) * P],
                                                v1[s][:, kb, :], start=(kb == 0), stop=(kb == TILES - 1))
                        ins.then_inc(ao_ps[s], 1)

                    yield
                    pe.wait_ge(aqT_sb[s], aqT_sb.at(k, 2))
                    pe.wait_ge(av_sb[s], av_sb.at(k, 0))
                    scores(0)
                    for hd in range(HEADS):
                        yield
                        if hd + 1 < HEADS:
                            scores(hd + 1)
                        yield
                        values(hd)
                    yield from out_projection(0, wout_s)

                def layer_attention(l):
                    def project(t, part, bank):
                        return pe.matmul(B4[:, bank, :], shT[s][:, t * P:(t + 1) * P],
                                         wqkv_s[l][:, part * INNER:(part + 1) * INNER], start=True, stop=True)

                    yield
                    pe.wait_ge(h_ready[s], h_ready.at(k, l))
                    for t in range(TILES):
                        ins = pe.transpose(B4[:, 3, t * P:(t + 1) * P], h[s][:, t, :], ident[:, :])
                    ins.then_inc(act_ps[s], 1)
                    yield
                    pe.wait_ge(act_sb[s], act_sb.at(k, 1 + 2 * l))
                    project(0, 0, 0)
                    project(0, 1, 1).then_inc(qk_ps[s], 1)
                    for t in range(TILES):
                        project(t, 2, 2 + t).then_inc(v_ps[s], 1)
                    yield
                    pe.wait_ge(qk_t[s], qk_t.at(k, l * TILES))
                    project(1, 0, 0)
                    project(1, 1, 1).then_inc(qk_ps[s], 1)
                    yield
                    pe.wait_ge(qk_n[s], qk_n.at(k, l * TILES))
                    for part in range(2):
                        pe.wait_ge(v_sb[s], v_sb.at(k, l * TILES + part))
                        transpose4(B4[:, 2 + part, :],
                                   qk[s][:, 0, part * INNER:(part + 1) * INNER]).then_inc(qkT_ps[s], 1)

                    def scores(u):
                        t, heads = unit(u)
                        if u >= 2:
                            pe.wait_ge(p_sb[s], p_sb.at(k, l * UNITS + u - 2))
                        kk = keys(t)
                        sc = B4[:, u % 2, :].rearrange("p (e n) -> p e n", e=2)
                        pe.matmul(sc[:, :, kk], identb[:, :],
                                  maskb[:, t, kk].unsqueeze(1).broadcast_to([P, 2, kk.stop - kk.start]),
                                  start=True, stop=False)
                        for e, hd in enumerate(heads):
                            ins = pe.matmul(sc[:, e, kk], qT[s][:, hd // 2, t * P:(t + 1) * P],
                                            kT[s][:, hd % 2, hd // 2, kk], start=False, stop=(e == 1))
                        ins.then_inc(s_ps[s], 1)

                    def turn(u):
                        t, _ = unit(u)
                        j = l * UNITS + u
                        pe.wait_ge(p_sb[s], p_sb.at(k, j))
                        if u >= 1:
                            pe.wait_ge(pT_sb[s], pT_sb.at(k, j - 1))
                        nb = len(blocks(t))
                        for e in range(2):
                            for b in blocks(t):
                                ins = pe.transpose(B4[:, 2, (e * nb + b) * P:(e * nb + b + 1) * P],
                                                   pb[s][2 * t + u % 2][:, e, b * P:(b + 1) * P], ident[:, :])
                        ins.then_inc(pT_ps[s], 1)

                    def values(u):
                        t, heads = unit(u)
                        pe.wait_ge(pT_sb[s], pT_sb.at(k, l * UNITS + u))
                        if u == PAIRS:
                            pe.wait_ge(o_sb[s], o_sb.at(k, l * TILES))
                        for e, hd in enumerate(heads):
                            for b in blocks(t):
                                ins = pe.matmul(B4[:, 3, hd * DH:(hd + 1) * DH], pT[s][u % 2][:, e, b, :],
                                                v8[s][:, b, hd * DH:(hd + 1) * DH],
                                                start=(b == 0), stop=(b == t))
                        ins.then_inc(pv_ps[s], 1)

                    yield
                    pe.wait_ge(qkT_sb[s], qkT_sb.at(k, l * TILES * 2 + 1))
                    pe.wait_ge(qk_t[s], qk_t.at(k, l * TILES + 1))
                    scores(0)
                    scores(1)
                    for u in range(UNITS):
                        yield
                        turn(u)
                        if u + 2 == TURN_AT:
                            yield
                            pe.wait_ge(qk_n[s], qk_n.at(k, l * TILES + 1))
                            for part in range(2):
                                pe.wait_ge(p_sb[s], p_sb.at(k, l * UNITS + u + part))
                                transpose4(B4[:, part, :],
                                           qk[s][:, 1, part * INNER:(part + 1) * INNER]).then_inc(qkT_ps[s], 1)
                        if u + 2 == TURN_AT:
                            yield
                            pe.wait_ge(qkT_sb[s], qkT_sb.at(k, l * TILES * 2 + 3))
                        if u + 2 < UNITS:
                            scores(u + 2)
                        yield
                        values(u)
                    yield from out_projection(1 + l, wo_s[l])

                def layer_ffn(l):
                    yield
                    pe.wait_ge(h_mid[s], h_mid.at(k, l))
                    for t in range(TILES):
                        dst = B4[:, 3, t * 64:(t + 1) * 64]
                        ins = pe.matmul(dst, shift[:, 0, :], h[s][:, t, 64:128], start=True, stop=(t == 0))
                        if t:
                            ins = pe.matmul(dst, shift[:, 1, :], h[s][:, t - 1, 64:128], start=False, stop=True)
                    ins.then_inc(sh_ps[s], 1)
                    yield
                    pe.wait_ge(hn_ready[s], hn_ready.at(k, l))
                    for t in range(TILES):
                        ins = pe.transpose(B4[:, 0, t * P:(t + 1) * P], y[s][:, t, :], ident[:, :])
                    ins.then_inc(act_ps[s], 1)
                    yield
                    pe.wait_ge(act_sb[s], act_sb.at(k, 2 + 2 * l))
                    for c, (c0, n) in enumerate(HID_CHUNKS):
                        for part in range(2):
                            ins = pe.matmul(B4[0:n, 1 + c, part * TOK:(part + 1) * TOK],
                                            w1_s[l][:, part * HID + c0:part * HID + c0 + n],
                                            actT[s][:, 0:TOK], start=True, stop=True)
                        ins.then_inc(f1_ps[s], 1)
                    yield
                    for t in range(TILES):
                        for c, (_, n) in enumerate(HID_CHUNKS):
                            yield
                            pe.wait_ge(hid_sb[s], hid_sb.at(k, l * NCH + c))
                            n += c == NCH - 1
                            ins = pe.matmul(B4[:, 0, t * P:(t + 1) * P], hid[s][0:n, c, t * P:(t + 1) * P],
                                            w2_s[l][0:n, c, :], start=(c == 0), stop=(c == NCH - 1))
                    ins.then_inc(f2_ps[s], 1)

                return attention_block, layer_attention, layer_ffn, nothing

            with pe.Fori(0, ROUNDS) as k:
                interleave(TURNS["tensor"], [whole_batch(*parts(s, k)) for s in range(STREAMS)])


def nothing():
    return iter(())


TURNS = {
    "gpsimd": (
        "010011001100110101010101"
    ),
    "scalar": (
        "0100011100001100001000110110111111000101000011011100100111001011011100110000111100011001"
        "11001101100100101101001011001100101011"
    ),
    "vector": (
        "0101000110011100100101010100010010100110001110110111010000001101011101101111001011000111"
        "01000110110101001011001001110011100010011100010101101010011100011100110011"
    ),
    "tensor": (
        "0101000101100000000010000000110111101100111111111011100110100001010011010010011001001111"
        "0011011001101010111100100110000011111010110101010100100101110011000111001001001100110001"
        "011110101010000110011111"
    ),
}


def whole_batch(attention_block, layer_attention, layer_ffn, last_norm):
    yield from attention_block()
    for l in range(DEPTH):
        yield from layer_attention(l)
        yield from layer_ffn(l)
    yield from last_norm()


def interleave(turns, batches):
    done = object()
    for steps in batches:
        next(steps)
    taken = [next(batches[int(s)], done) for s in turns]
    assert taken.count(done) == len(batches), "steps without a turn"





_INS = ['L0_attn_x', 'L0_attn_norm_g', 'L0_attn_Wq', 'L0_attn_Wkv', 'L0_attn_Wout', 'L0_attn_out_norm_g',
        'L0_ffn_wqkv', 'L0_ffn_q_scale', 'L0_ffn_k_scale', 'L0_ffn_wo', 'L0_ffn_ln_g', 'L0_ffn_ln_b',
        'L0_ffn_w1', 'L0_ffn_b1', 'L0_ffn_w2', 'L0_ffn_b2']
_OUTS = [((16, 256, 128), 'float32')]


def kernel(**inputs):
    import numpy as _np
    import concourse.bacc as _bacc
    from concourse import mybir as _mybir
    from concourse.bass_utils import run_bass_kernel_spmd as _run

    nc = _bacc.Bacc("TRN2", target_bir_lowering=False, num_devices=1)
    given = {name: _np.ascontiguousarray(inputs[name]) for name in _INS}
    given.update(shape_constants())
    arrays, args = {}, []
    for name, a in given.items():
        arrays[f"in_{name}_dram"] = a
        args.append(nc.dram_tensor(f"in_{name}_dram", a.shape, _mybir.dt.from_np(a.dtype), kind="ExternalInput").ap())
    for i, (shape, dtype) in enumerate(_OUTS):
        dt = _mybir.dt.from_np(_np.dtype(dtype))
        args.append(nc.dram_tensor(f"out_{i}_dram", shape, dt, kind="ExternalOutput").ap())
    sandwich_kernel(nc, *args)
    r = _run(nc, [arrays], core_ids=[0])
    got = tuple(r.results[0][f"out_{i}_dram"] for i in range(len(_OUTS)))
    return got[0]
```

```python
from contextlib import ExitStack
from itertools import chain

import numpy as np

import concourse.bass as bass
from concourse import mybir
from concourse.alu_op_type import AluOpType as ALU

F32 = mybir.dt.float32
BF16 = mybir.dt.bfloat16
ACT = mybir.ActivationFunctionType
AX_X = mybir.AxisListType.X

P = 128
TOK = 256
TILES = TOK // P
DIM = 128
HEADS = 8
DH = 64
INNER = HEADS * DH
PAIRS = HEADS // 2
WINDOW = 64
DEPTH = 2
HID = int(DIM * 4 * 2 / 3)
HID_CHUNKS = [(c, min(P, HID - c)) for c in range(0, HID, P)]
NCH = len(HID_CHUNKS)
HID_LAST = HID_CHUNKS[-1][1]
EPS = 1e-5
QK_SCALE = 8.0
SIM_SCALE = 16.0
NEG = -1e30
STREAMS = 2
LOADS_TO_PREPARE = 11 + 3 * DEPTH
LOADS = 7 + DEPTH
PRESETS = 3 + 7 * STREAMS
BLOCK_LINKS, ATTENTION_LINKS, FFN_LINKS, LAST_LINKS = 27, 4, 6, 6
UNITS = TILES * PAIRS
NORM_AT = 1
TURN_AT = 4


def shape_constants():
    half = np.arange(0, DH, 2, dtype=np.float32)
    inv_freq = (1.0 / np.float32(10000.0) ** (half / np.float32(DH))).astype(np.float32)
    t = np.arange(TOK, dtype=np.float32)
    freqs = t[:, None] * inv_freq[None, :]
    freqs = np.concatenate([freqs, freqs], axis=-1)
    base = (half + np.float32(0.4 * DH)) / np.float32(1.4 * DH)
    power = (t - TOK // 2) / np.float32(WINDOW // 2)
    scale = base[None, :] ** power[:, None]
    scale = np.concatenate([scale, scale], axis=-1)
    cos, sin = np.cos(freqs), np.sin(freqs)
    sign = np.where(np.arange(DH) < DH // 2, -1.0, 1.0).astype(np.float32)
    rot = np.stack([np.stack([cos * scale * QK_SCALE, sign * sin * scale * QK_SCALE], 1),
                    np.stack([cos / scale, sign * sin / scale], 1)], 1).astype(np.float32)
    rot = rot.reshape(TILES, P, 2, 2, DH).transpose(1, 0, 2, 3, 4)
    i, j = np.arange(TOK)[:, None], np.arange(TOK)[None, :]
    mask = np.where((i < j) | (i > j + WINDOW), NEG, 0.0).astype(np.float32)
    mask = mask.reshape(TILES, P, TOK).transpose(1, 0, 2)
    shift = np.zeros((P, 2, P), np.float32)
    shift[np.arange(P - 1), 0, np.arange(1, P)] = 1.0
    shift[P - 1, 1, 0] = 1.0
    return {
        "rot": np.ascontiguousarray(rot.reshape(P, -1)),
        "mask": np.ascontiguousarray(mask.reshape(P, -1)),
        "ident": np.eye(P, dtype=np.float32),
        "shift": shift.reshape(P, -1),
    }


def sandwich_kernel(nc: bass.Bass, x, norm_g, Wq, Wkv, Wout, out_norm_g, wqkv, q_scale, k_scale, wo,
                    ln_g, ln_b, w1, b1, w2, b2, rot_c, mask_c, ident_c, shift_c, out):
    B = x.shape[0]
    ROUNDS = B // STREAMS

    with ExitStack() as ctx:
        def sb(name, shape, dt=F32):
            return ctx.enter_context(nc.sbuf_tensor(name, shape, dt))

        def sem(name):
            return ctx.enter_context(nc.semaphore(name))

        def per_stream(make):
            return [make(s) for s in range(STREAMS)]

        ident = sb("ident", [P, P])
        identb = sb("identb", [P, P], BF16)
        shift = sb("shift", [P, 2, P])
        maskb = sb("maskb", [P, TILES, TOK], BF16)
        rot = sb("rot", [P, TILES, 2, 2, DH])
        qks = sb("qks", [P, DEPTH, 2, DH])
        tab = [sb(f"tab{l}", [P, TILES, 2, 2, DH]) for l in range(DEPTH)]
        ng = sb("ng", [P, 1])
        outg = sb("outg", [P, DIM])
        wq_s = sb("wq_s", [P, INNER])
        wkv_s = sb("wkv_s", [P, 2 * DH])
        wout_s = sb("wout_s", [P, PAIRS, DIM])
        wqkv_all = sb("wqkv_s", [P, DEPTH, 3 * INNER])
        wo_all = sb("wo_s", [P, DEPTH, PAIRS, DIM])
        w1_all = sb("w1_s", [P, DEPTH, 2 * HID])
        w2_all = sb("w2_s", [P, DEPTH, NCH, DIM])
        wqkv_s, wo_s, w1_s, w2_s = ([w[:, l] for l in range(DEPTH)] for w in (wqkv_all, wo_all, w1_all, w2_all))
        lng = sb("lng", [P, DEPTH])
        lnb = sb("lnb", [P, DEPTH])
        b1c = sb("b1c", [P, DEPTH, 2, NCH])
        b1f = sb("b1f", [P, DEPTH, 2, NCH])
        halfpow = sb("halfpow", [P, 2 * HEADS])
        floor = sb("floor", [P, HEADS + 1])

        xin = per_stream(lambda s: sb(f"xin{s}", [P, TILES, DIM]))
        x1 = per_stream(lambda s: sb(f"x1_{s}", [P, TILES, DIM]))
        y = per_stream(lambda s: sb(f"y{s}", [P, TILES, DIM]))
        z = per_stream(lambda s: sb(f"z{s}", [P, TILES, DIM]))
        h = per_stream(lambda s: sb(f"h{s}", [P, TILES, DIM]))
        fin = per_stream(lambda s: sb(f"fin{s}", [P, TILES, DIM]))
        st = per_stream(lambda s: sb(f"st{s}", [P, TILES, 2, 6]))
        aside = per_stream(lambda s: sb(f"aside{s}", [P, 1]))
        mv = per_stream(lambda s: sb(f"mv{s}", [P, TILES, 2]))
        arg = per_stream(lambda s: sb(f"arg{s}", [P, TILES]))
        rstd = per_stream(lambda s: sb(f"rstd{s}", [P, TILES]))
        actT = per_stream(lambda s: sb(f"actT{s}", [P, TOK + 1]))
        shT = per_stream(lambda s: sb(f"shT{s}", [P, TOK + 1]))
        sq = per_stream(lambda s: sb(f"sq{s}", [P, 2, 2 * INNER]))
        maskf = sq[1][:, 0, 0:TILES * TOK].rearrange("p (a n) -> p a n", a=TILES)
        w1_raw = sq[0][:, :, 0:2 * HID]
        ss = per_stream(lambda s: sb(f"ss{s}", [P, TILES, 2 * HEADS]))
        rn = per_stream(lambda s: sb(f"rn{s}", [P, TILES, 2 * HEADS]))
        qk = per_stream(lambda s: sb(f"qk{s}", [P, TILES, 2 * INNER]))
        t1 = per_stream(lambda s: sb(f"t1_{s}", [P, TILES, 2 * INNER]))
        t2 = per_stream(lambda s: sb(f"t2_{s}", [P, TILES, 2 * INNER]))
        qT = per_stream(lambda s: sb(f"qT{s}", [P, PAIRS, TOK]))
        kT = per_stream(lambda s: sb(f"kT{s}", [P, 2, PAIRS, TOK]))
        v1 = per_stream(lambda s: sb(f"v1_{s}", [P, TILES, P]))
        v8 = per_stream(lambda s: sb(f"v8_{s}", [P, TILES, INNER]))
        pb = per_stream(lambda s: [sb(f"pb{s}_{b}", [P, 2, TOK]) for b in range(4)])
        pT = per_stream(lambda s: [sb(f"pT{s}_{b}", [P, 2, 2, P]) for b in range(2)])
        nmax = per_stream(lambda s: sb(f"nmax{s}", [P, UNITS, 2]))
        psm = per_stream(lambda s: sb(f"psm{s}", [P, TILES, HEADS]))
        rsm = per_stream(lambda s: sb(f"rsm{s}", [P, TILES, HEADS]))
        o = per_stream(lambda s: sb(f"o{s}", [P, TILES, INNER]))
        oT = per_stream(lambda s: sb(f"oT{s}", [P, PAIRS, TOK]))
        gate = per_stream(lambda s: sb(f"gate{s}", [P, NCH, TOK]))
        hid = per_stream(lambda s: sb(f"hid{s}", [P, NCH, TOK]))

        ps = per_stream(lambda s: ctx.enter_context(nc.psum_tensor(f"ps{s}", [P, 4, 512], F32)))

        s_raw = sem("weights_to_prepare_loaded")
        s_w = sem("other_weights_loaded")
        s_wa = sem("weights_ready_dve")
        s_wb = sem("bf16_constants_ready")
        s_wp = sem("bias_product_ready")
        s_init = sem("presets_done")
        s_ld = [sem(f"x_loaded{s}") for s in range(STREAMS)]
        s_st = [sem(f"out_stored{s}") for s in range(STREAMS)]

        class Signal:

            def __init__(self, name, per):
                self.per = per
                self.sems = [sem(f"{name}{s}") for s in range(STREAMS)]

            def __getitem__(self, s):
                return self.sems[s]

            def at(self, k, n):
                return k * self.per + (n + 1)

        xfree = Signal("x_consumed", 1)
        own_block = Signal("dve_own_block", BLOCK_LINKS)
        own_attention = Signal("dve_own_attention", DEPTH * ATTENTION_LINKS)
        own_ffn = Signal("dve_own_ffn", DEPTH * FFN_LINKS)
        own_last = Signal("dve_own_last", LAST_LINKS)
        var_ready = Signal("variance_ready", 4 + DEPTH)
        rstd_ready = Signal("rstd_ready", 4 + DEPTH)
        y_ready = Signal("normed_ready", 1)
        act_ps = Signal("actT_in_psum", 1 + 2 * DEPTH)
        act_sb = Signal("actT_in_sbuf", 1 + 2 * DEPTH)
        aq_ps = Signal("a_qkv_in_psum", 3)
        aq_sq = Signal("a_squares_ready", 3)
        av_sb = Signal("a_v_ready", 1)
        ss_ready = Signal("norms_squared_ready", TILES * (1 + DEPTH))
        rn_ready = Signal("inverse_norms_ready", TILES * (1 + DEPTH))
        aqk_n = Signal("a_qk_normed", 3)
        aqT_ps = Signal("a_qkT_in_psum", 3)
        aqT_sb = Signal("a_qkT_in_sbuf", 3)
        as_ps = Signal("a_scores_in_psum", HEADS)
        ap_sb = Signal("a_probs_ready", HEADS)
        ao_ps = Signal("a_head_out_in_psum", HEADS)
        ao_sb = Signal("a_out_normed", 2)
        oT_ps = Signal("oT_in_psum", TILES * (1 + DEPTH))
        oT_sb = Signal("oT_in_sbuf", TILES * (1 + DEPTH))
        proj_ps = Signal("out_projection_in_psum", 1 + DEPTH)
        h_ready = Signal("residual_ready", 1 + DEPTH)
        h_mid = Signal("residual_after_attention", DEPTH)
        qk_ps = Signal("qk_in_psum", TILES * DEPTH)
        v_ps = Signal("v_in_psum", TILES * DEPTH)
        v_sb = Signal("v_in_sbuf", TILES * DEPTH)
        qk_sq = Signal("qk_squares_ready", 2 * TILES * DEPTH)
        qk_t = Signal("rotary_products_ready", TILES * DEPTH)
        qk_rot = Signal("rotary_sum_ready", TILES * DEPTH)
        qk_n = Signal("qk_rotated_normed", TILES * DEPTH)
        qkT_ps = Signal("qkT_in_psum", 2 * TILES * DEPTH)
        qkT_sb = Signal("qkT_in_sbuf", 2 * TILES * DEPTH)
        s_ps = Signal("scores_in_psum", UNITS * DEPTH)
        mx_ready = Signal("negated_max_ready", UNITS * DEPTH)
        p_sb = Signal("probs_ready", UNITS * DEPTH)
        pT_ps = Signal("probsT_in_psum", UNITS * DEPTH)
        pT_even = Signal("even_probsT_in_sbuf", UNITS // 2 * DEPTH)
        pT_odd = Signal("odd_probsT_in_sbuf", UNITS // 2 * DEPTH)
        pv_ps = Signal("head_out_in_psum", UNITS * DEPTH)
        o_sb = Signal("out_normed", TILES * DEPTH)
        sh_ps = Signal("shifted_half_in_psum", DEPTH)
        hn_ready = Signal("shifted_normed_ready", DEPTH)
        f1_ps = Signal("hidden_in_psum", NCH * DEPTH)
        gate_sb = Signal("gate_ready", NCH * DEPTH)
        hid_sb = Signal("hidden_ready", NCH * DEPTH)
        f2_ps = Signal("ffn_out_in_psum", DEPTH)
        fin_ready = Signal("result_ready", 1)

        def rows(n):
            return slice(64 * n, 64 * n + 64)

        def keys(t):
            return slice(max(t * P - WINDOW, 0), (t + 1) * P)

        def unit(u):
            t, n = divmod(u, PAIRS)
            return t, [4 * (n // 2) + n % 2, 4 * (n // 2) + 2 + n % 2]

        def blocks(t):
            return range(t + 1)

        def turned_probs(s, u):
            nb = len(blocks(unit(u)[0]))
            return (ps[s][:, 2, 0:2 * nb * P].rearrange("p (e b n) -> p e b n", e=2, b=nb),
                    pT[s][u % 2][:, :, 0:nb, :])

        x_v = x.rearrange("b (t p) d -> b p t d", p=P)
        out_v = out.rearrange("b (t p) d -> b p t d", p=P)

        block = ctx.enter_context(nc.Block())

        @block.sync
        def _(sp):
            def load(dst, src, signal, by_element=False):
                sp.dma_start(dst, src, allow_slow_non_contiguous=by_element).then_inc(signal, 16)

            for s in range(STREAMS):
                sp.dma_start(xin[s][:, :, :], x_v[s]).then_inc(s_ld[s], 16)
                sp.sem_inc(s_st[s], 16)
            load(lnb[:, :], ln_b.rearrange("l p -> p l"), s_raw, by_element=True)
            load(w1_raw, w1.rearrange("l p n -> p l n"), s_raw)
            load(ident[:, :], ident_c, s_raw)
            load(maskf, mask_c.rearrange("p (a n) -> p a n", a=TILES), s_raw)
            load(rot[:, :, :, :, :], rot_c.rearrange("p (t a b d) -> p t a b d", t=TILES, a=2, b=2), s_raw)
            load(qks[:, :, 0, :], q_scale.partition_broadcast(P), s_raw)
            load(qks[:, :, 1, :], k_scale.partition_broadcast(P), s_raw)
            load(ng[:, :], norm_g.rearrange("(p a) -> p a", a=1), s_raw)
            load(lng[:, :], ln_g.rearrange("l p -> p l"), s_raw, by_element=True)
            load(wq_s[:, :], Wq, s_raw)
            load(wkv_s[:, :], Wkv, s_raw)
            whole = (NCH - 1) * P
            b1_v = b1.rearrange("l (a n) -> l a n", a=2)
            for l in range(DEPTH):
                for part in range(2):
                    load(b1c[:, l, part, 0:NCH - 1],
                         b1_v[l, part, 0:whole].rearrange("(c p) -> p c", p=P), s_raw, by_element=True)
                load(b1c[0:HID_LAST, l, :, NCH - 1], b1_v[l, :, whole:HID].rearrange("a p -> p a"), s_raw,
                     by_element=True)
            load(wqkv_all[:, :, :], wqkv.rearrange("l p n -> p l n"), s_w)
            load(wout_s[:, :, :], Wout.rearrange("(c p) n -> p c n", p=P), s_w)
            load(outg[:, :], out_norm_g.partition_broadcast(P), s_w)
            load(shift[:, :, :], shift_c.rearrange("p (a n) -> p a n", a=2), s_w)
            load(wo_all[:, :, :, :], wo.rearrange("l (c p) n -> p l c n", p=P), s_w)
            for l in range(DEPTH):
                load(w2_s[l][:, 0:NCH - 1, :], w2[l, 0:whole, :].rearrange("(c p) n -> p c n", p=P), s_w)
            load(w2_all[0:HID_LAST, :, NCH - 1, :], w2[:, whole:HID, :].rearrange("l p n -> p l n"), s_w)
            load(w2_all[HID_LAST:HID_LAST + 1, :, NCH - 1, :], b2.unsqueeze(0), s_w)

            def store(s, k, b):
                sp.wait_ge(fin_ready[s], fin_ready.at(k, 0))
                sp.dma_start(out_v[b], fin[s][:, :, :]).then_inc(s_st[s], 16)

            with sp.Fori(0, ROUNDS - 1) as k:
                for s in range(STREAMS):
                    sp.wait_ge(xfree[s], xfree.at(k, 0))
                    sp.dma_start(xin[s][:, :, :], x_v[(k + 1) * STREAMS + s]).then_inc(s_ld[s], 16)
                for s in range(STREAMS):
                    store(s, k, k * STREAMS + s)
            for s in range(STREAMS):
                store(s, ROUNDS - 1, (ROUNDS - 1) * STREAMS + s)
            for s in range(STREAMS):
                sp.wait_ge(s_st[s], 16 * (ROUNDS + 1))

        @block.gpsimd
        def _(pool):
            pool.memset(halfpow[:, :], -0.5).then_inc(s_init, 1)
            pool.memset(floor[:, 0:HEADS], (1e-12 / SIM_SCALE) ** 2).then_inc(s_init, 1)
            pool.memset(floor[:, HEADS:HEADS + 1], 1e-24).then_inc(s_init, 1)
            for s in range(STREAMS):
                pool.memset(v1[s][:, :, DH:DH + 1], 1.0).then_inc(s_init, 1)
                pool.memset(v1[s][:, :, DH + 1:P], 0.0).then_inc(s_init, 1)
                pool.memset(kT[s][:, :, :, :], 0.0).then_inc(s_init, 1)
                pool.memset(shT[s][:, :], 0.0).then_inc(s_init, 1)
                pool.memset(hid[s][:, :, :], 1.0).then_inc(s_init, 1)
                for b in range(2, 4):
                    pool.memset(pb[s][b][:, :, 0:WINDOW], 0.0).then_inc(s_init, 1)
            pool.wait_ge(s_init, PRESETS)

            def parts(s, k):
                def norm_rstd(n):
                    pool.wait_ge(var_ready[s], var_ready.at(k, n))
                    pool.tensor_tensor(rstd[s][:, :], arg[s][:, :], halfpow[:, 0:TILES],
                                       ALU.pow).then_inc(rstd_ready[s], 1)

                def attention_block():
                    yield
                    norm_rstd(0)
                    for t in range(TILES):
                        yield
                        pool.wait_ge(ss_ready[s], ss_ready.at(k, t))
                        pool.tensor_tensor(rn[s][:, t, 0:HEADS + 1], ss[s][:, t, 0:HEADS + 1],
                                           halfpow[:, 0:HEADS + 1], ALU.pow).then_inc(rn_ready[s], 1)
                    for n in range(2):
                        yield
                        norm_rstd(1 + n)

                def layer_attention(l):
                    for t in range(TILES):
                        j = l * TILES + t
                        yield
                        pool.wait_ge(ss_ready[s], ss_ready.at(k, TILES + j))
                        pool.tensor_tensor(rn[s][:, t, :], ss[s][:, t, :], halfpow[:, 0:2 * HEADS],
                                           ALU.pow).then_inc(rn_ready[s], 1)

                def layer_ffn(l):
                    yield
                    norm_rstd(3 + l)

                def last_norm():
                    yield
                    norm_rstd(3 + DEPTH)

                return attention_block, layer_attention, layer_ffn, last_norm

            run_streams(pool, ROUNDS, "gpsimd", parts)

        @block.scalar
        def _(act):
            act.wait_ge(s_init, PRESETS)
            act.wait_ge(s_raw, 16 * LOADS_TO_PREPARE)
            act.activation(identb[:, :], ident[:, :], ACT.Copy).then_inc(s_wb, 1)
            act.activation(maskb[:, :, :], maskf, ACT.Copy).then_inc(s_wb, 1)
            act.wait_ge(s_wb, 2)
            act.wait_ge(s_wa, 2)
            copy, square = ACT.Copy, ACT.Square

            def parts(s, k):
                B4 = ps[s]

                def out_T(n):
                    for t in range(TILES):
                        yield
                        act.wait_ge(oT_ps[s], oT_ps.at(k, n * TILES + t))
                        act.activation(oT[s][:, :, t * P:(t + 1) * P],
                                       B4[:, t, :].rearrange("p (c n) -> p c n", c=PAIRS),
                                       copy).then_inc(oT_sb[s], 1)

                def attention_block():
                    yield
                    act.wait_ge(act_ps[s], act_ps.at(k, 0))
                    act.activation(actT[s][:, 0:TOK], B4[:, 3, 0:TOK], copy).then_inc(act_sb[s], 1)
                    yield
                    act.wait_ge(aq_ps[s], aq_ps.at(k, 0))
                    kv = B4[:, 2, 0:TILES * 2 * DH].rearrange("p (t n) -> p t n", t=TILES)
                    act.activation(sq[s][:, :, INNER:INNER + DH], kv[:, :, 0:DH], square).then_inc(aq_sq[s], 1)
                    act.activation(v1[s][:, :, 0:DH], kv[:, :, DH:2 * DH], copy).then_inc(av_sb[s], 1)
                    for t in range(TILES):
                        yield
                        act.wait_ge(aq_ps[s], aq_ps.at(k, 1 + t))
                        act.activation(sq[s][:, t, 0:INNER], B4[:, t, :], square).then_inc(aq_sq[s], 1)
                    for t, bank in ((0, 3), (1, 0)):
                        yield
                        act.wait_ge(aqT_ps[s], aqT_ps.at(k, t))
                        act.activation(qT[s][:, :, t * P:(t + 1) * P],
                                       B4[:, bank, :].rearrange("p (c n) -> p c n", c=PAIRS),
                                       copy).then_inc(aqT_sb[s], 1)
                    yield
                    act.wait_ge(aqT_ps[s], aqT_ps.at(k, 2))
                    for e in range(2):
                        ins = act.activation(kT[s][rows(e), e, 0, :], B4[rows(e), 1, 0:TOK], copy)
                    ins.then_inc(aqT_sb[s], 1)
                    for hd in range(HEADS):
                        yield
                        act.wait_ge(as_ps[s], as_ps.at(k, hd))
                        if hd >= 2:
                            act.wait_ge(ao_ps[s], ao_ps.at(k, hd - 2))
                        act.activation(pb[s][hd % 2][:, :, :].rearrange("p a n -> p (a n)"),
                                       B4[:, hd % 2, :], ACT.Exp, scale=SIM_SCALE).then_inc(ap_sb[s], 1)
                    yield from out_T(0)

                def layer_attention(l):
                    yield
                    act.wait_ge(act_ps[s], act_ps.at(k, 1 + 2 * l))
                    act.activation(shT[s][0:64, 0:TOK], B4[0:64, 3, 0:TOK], copy)
                    act.activation(shT[s][64:128, 1:TOK + 1], B4[64:128, 3, 0:TOK], copy).then_inc(act_sb[s], 1)
                    for t in range(TILES):
                        j = l * TILES + t
                        yield
                        act.wait_ge(qk_ps[s], qk_ps.at(k, j))
                        for part in range(2):
                            act.activation(sq[s][:, t, part * INNER:(part + 1) * INNER], B4[:, part, :],
                                           square).then_inc(qk_sq[s], 1)
                        yield
                        act.wait_ge(v_ps[s], v_ps.at(k, j))
                        act.activation(v8[s][:, t, :], B4[:, 2 + t, :], copy).then_inc(v_sb[s], 1)

                    def turned(t, bank):
                        q_ps, k_ps = (B4[:, bank + part, :].rearrange("p (c n) -> p c n", c=PAIRS)
                                      for part in range(2))
                        yield
                        act.wait_ge(qkT_ps[s], qkT_ps.at(k, (l * TILES + t) * 2))
                        act.activation(qT[s][:, :, t * P:(t + 1) * P], q_ps, copy).then_inc(qkT_sb[s], 1)
                        yield
                        act.wait_ge(qkT_ps[s], qkT_ps.at(k, (l * TILES + t) * 2 + 1))
                        for e in range(2):
                            ins = act.activation(kT[s][rows(e), e, :, t * P:(t + 1) * P], k_ps[rows(e)], copy)
                        ins.then_inc(qkT_sb[s], 1)

                    yield from turned(0, 2)

                    def turned_unit(u):
                        j = l * UNITS + u
                        act.wait_ge(pT_ps[s], pT_ps.at(k, j))
                        if u >= 2:
                            act.wait_ge(pv_ps[s], pv_ps.at(k, j - 2))
                        src, dst = turned_probs(s, u)
                        act.activation(dst, src, copy).then_inc(pT_odd[s], 1)

                    for u in range(UNITS):
                        t, heads = unit(u)
                        j = l * UNITS + u
                        if u == TURN_AT:
                            yield from turned(1, 0)
                        yield
                        act.wait_ge(mx_ready[s], mx_ready.at(k, j))
                        if u >= 2:
                            act.wait_ge(pT_ps[s], pT_ps.at(k, j - 2))
                        for e, hd in enumerate(heads):
                            ins = act.activation(pb[s][2 * t + u % 2][:, e, keys(t)],
                                                 B4[:, u % 2, :].rearrange("p (e n) -> p e n", e=2)[:, e, keys(t)],
                                                 ACT.Exp, bias=nmax[s][:, u, e:e + 1],
                                                 accum_out=psm[s][:, t, hd:hd + 1])
                        ins.then_inc(p_sb[s], 1)
                        if u and u % 2 == 0:
                            yield
                            turned_unit(u - 1)
                    yield
                    turned_unit(UNITS - 1)
                    yield from out_T(1 + l)

                def layer_ffn(l):
                    yield
                    act.wait_ge(act_ps[s], act_ps.at(k, 2 + 2 * l))
                    act.activation(actT[s][:, 0:TOK], B4[:, 0, 0:TOK], copy).then_inc(act_sb[s], 1)
                    for c, (_, n) in enumerate(HID_CHUNKS):
                        yield
                        act.wait_ge(f1_ps[s], f1_ps.at(k, l * NCH + c))
                        act.activation(gate[s][0:n, c, :], B4[0:n, 1 + c, TOK:2 * TOK], ACT.Gelu,
                                       bias=b1f[0:n, l, 1, c:c + 1]).then_inc(gate_sb[s], 1)

                return attention_block, layer_attention, layer_ffn, nothing

            run_streams(act, ROUNDS, "scalar", parts)

        @block.vector
        def _(dve):
            dve.wait_ge(s_raw, 16 * LOADS_TO_PREPARE)
            dve.tensor_scalar(wq_s[:, :], wq_s[:, :], ng[:, 0:1], None, ALU.mult)
            dve.tensor_scalar(wkv_s[:, :], wkv_s[:, :], ng[:, 0:1], None, ALU.mult)
            for l in range(DEPTH):
                dve.tensor_scalar(w1_s[l], w1_raw[:, l, :], lng[:, l:l + 1], None, ALU.mult)
                for part in range(2):
                    qs = qks[:, l, part, :].unsqueeze(1).broadcast_to([P, TILES, DH])
                    dve.tensor_tensor(tab[l][:, :, part, 0, :], rot[:, :, part, 0, :], qs, ALU.mult)
                    for a in range(2):
                        this, other = (slice(DH // 2 * x, DH // 2 * (x + 1)) for x in (a, 1 - a))
                        ins = dve.tensor_tensor(tab[l][:, :, part, 1, this], rot[:, :, part, 1, this],
                                                qs[:, :, other], ALU.mult)
            ins.then_inc(s_wa, 1)
            dve.wait_ge(s_wp, 1)
            for l in range(DEPTH):
                for part in range(2):
                    for c, (_, n) in enumerate(HID_CHUNKS):
                        col = (l * 2 + part) * NCH + c
                        ins = dve.tensor_tensor(b1f[0:n, l, part, c:c + 1], b1c[0:n, l, part, c:c + 1],
                                                ps[0][0:n, 0, col:col + 1], ALU.add)
            ins.then_inc(s_wa, 1)
            dve.wait_ge(s_init, PRESETS)
            dve.wait_ge(s_w, 16 * LOADS)

            def parts(s, k):
                B4 = ps[s]
                links = []

                def link(*instructions):
                    own = links[0]
                    for ins in instructions:
                        ins.then_inc(own[s], 1)
                        links[1] += 1
                    dve.wait_ge(own[s], own.at(k, links[1] - 1))

                def stats(pieces):
                    link(*[dve.bn_stats(st[s][:, t, a, :], piece)
                           for t in range(TILES) for a, piece in enumerate(pieces(t))])
                    dve.memset(aside[s][:, :], 0.0)
                    link(*[dve.bn_aggr(mv[s][:, t, :], st[s][:, t, 0:len(pieces(t)), :])
                           for t in range(TILES)])

                def variance(times=1.0, plus=EPS):
                    dve.tensor_scalar(arg[s][:, :], mv[s][:, :, 1], times, plus,
                                      ALU.mult, ALU.add).then_inc(var_ready[s], 1)

                def normed(dst, src, t):
                    return dve.tensor_scalar(dst, src, mv[s][:, t, 0:1], rstd[s][:, t:t + 1],
                                             ALU.subtract, ALU.mult)

                def attention_block():
                    yield
                    links[:] = own_block, 0
                    dve.wait_ge(s_ld[s], k * 16 + 16)
                    stats(lambda t: [xin[s][:, t, :]])
                    variance(1.0 + EPS, EPS * EPS)
                    yield
                    dve.wait_ge(rstd_ready[s], rstd_ready.at(k, 0))
                    for t in range(TILES):
                        ins = normed(y[s][:, t, :], xin[s][:, t, :], t)
                    ins.then_inc(y_ready[s], 1)
                    for t in range(TILES):
                        yield
                        dve.wait_ge(aq_sq[s], aq_sq.at(k, 1 + t))
                        link(dve.tensor_reduce(ss[s][:, t, 0:HEADS + 1], sq[s][:, t, 0:INNER + DH]
                                               .rearrange("p (h d) -> p h d", d=DH), AX_X, ALU.add))
                        dve.tensor_tensor(ss[s][:, t, 0:HEADS + 1], ss[s][:, t, 0:HEADS + 1], floor[:, :],
                                          ALU.max).then_inc(ss_ready[s], 1)
                    for t in range(TILES):
                        yield
                        dve.wait_ge(rn_ready[s], rn_ready.at(k, t))
                        dve.tensor_tensor(
                            qk[s][:, t, 0:INNER].rearrange("p (h d) -> p h d", d=DH),
                            B4[:, t, :].rearrange("p (h d) -> p h d", d=DH),
                            rn[s][:, t, 0:HEADS].unsqueeze(2).broadcast_to([P, HEADS, DH]),
                            ALU.mult).then_inc(aqk_n[s], 1)
                    yield
                    dve.wait_ge(av_sb[s], av_sb.at(k, 0))
                    for t in range(TILES):
                        ins = dve.tensor_scalar(
                            qk[s][:, t, INNER:INNER + P].rearrange("p (a d) -> p a d", a=2),
                            B4[:, 2, t * 2 * DH:t * 2 * DH + DH].unsqueeze(1).broadcast_to([P, 2, DH]),
                            rn[s][:, t, HEADS:HEADS + 1], None, ALU.mult)
                    ins.then_inc(aqk_n[s], 1)
                    for quad in range(2):
                        yield
                        dve.wait_ge(ao_ps[s], ao_ps.at(k, 4 * quad + 3))
                        o4 = [B4[:, 2 + t, :].rearrange("p (h d) -> p h d", h=4) for t in range(TILES)]
                        hs = slice(4 * quad, 4 * quad + 4)
                        link(*[dve.reciprocal(rsm[s][:, t, hs], o4[t][:, :, DH]) for t in range(TILES)])
                        for t in range(TILES):
                            ins = dve.tensor_tensor(
                                o[s][:, t, :].rearrange("p (h d) -> p h d", d=DH)[:, hs, :], o4[t][:, :, 0:DH],
                                rsm[s][:, t, hs].unsqueeze(2).broadcast_to([P, 4, DH]), ALU.mult)
                        ins.then_inc(ao_sb[s], 1)
                    yield
                    dve.wait_ge(proj_ps[s], proj_ps.at(k, 0))
                    pr = B4[:, 2, 0:TOK].rearrange("p (t n) -> p t n", t=TILES)
                    stats(lambda t: [pr[:, t, :]])
                    link(dve.tensor_scalar(arg[s][:, :], mv[s][:, :, 1], EPS, EPS, ALU.add, ALU.mult),
                         *[dve.scalar_tensor_tensor(out=z[s][:, t, :], in0=pr[:, t, :], scalar=mv[s][:, t, 0:1],
                                                    in1=outg[:, :], op0=ALU.subtract, op1=ALU.mult)
                           for t in range(TILES)])
                    stats(lambda t: [z[s][:, t, :]])
                    dve.tensor_tensor(arg[s][:, :], arg[s][:, :], mv[s][:, :, 1], ALU.add).then_inc(var_ready[s], 1)
                    yield
                    dve.wait_ge(rstd_ready[s], rstd_ready.at(k, 1))
                    link(*[normed(y[s][:, t, :], z[s][:, t, :], t) for t in range(TILES)])
                    dve.tensor_tensor(x1[s][:, :, :], xin[s][:, :, :], y[s][:, :, :],
                                      ALU.add).then_inc(xfree[s], 1)
                    dve.wait_ge(xfree[s], xfree.at(k, 0))
                    stats(lambda t: [x1[s][:, t, :]])
                    variance()
                    yield
                    dve.wait_ge(rstd_ready[s], rstd_ready.at(k, 2))
                    for t in range(TILES):
                        ins = normed(h[s][:, t, :], x1[s][:, t, :], t)
                    ins.then_inc(h_ready[s], 1)

                def layer_attention(l):
                    def normed_qk(t):
                        j = l * TILES + t
                        dve.wait_ge(qk_rot[s], qk_rot.at(k, j))
                        dve.wait_ge(rn_ready[s], rn_ready.at(k, TILES + j))
                        dve.tensor_tensor(
                            qk[s][:, t, :].rearrange("p (h d) -> p h d", d=DH),
                            t1[s][:, t, :].rearrange("p (h d) -> p h d", d=DH),
                            rn[s][:, t, :].unsqueeze(2).broadcast_to([P, 2 * HEADS, DH]),
                            ALU.mult).then_inc(qk_n[s], 1)

                    def rotary_products(t):
                        j = l * TILES + t
                        dve.wait_ge(qk_ps[s], qk_ps.at(k, j))
                        shape = [P, HEADS, 2, DH // 2]
                        for part in range(2):
                            half = B4[:, part, :].rearrange("p (h a d) -> p h a d", a=2, d=DH // 2)
                            cs, sn = (tab[l][:, t, part, a, :].rearrange("p (a d) -> p a d", a=2)
                                      .unsqueeze(1).broadcast_to(shape) for a in range(2))
                            dst = [tt[s][:, t, part * INNER:(part + 1) * INNER]
                                   .rearrange("p (h a d) -> p h a d", a=2, d=DH // 2) for tt in (t1, t2)]
                            dve.wait_ge(qk_sq[s], qk_sq.at(k, 2 * j + part))
                            dve.tensor_tensor(dst[0], half, cs, ALU.mult)
                            ins = dve.tensor_tensor(dst[1], half[:, :, ::-1, :], sn, ALU.mult)
                        ins.then_inc(qk_t[s], 1)

                    def squared_norms(t):
                        link(dve.tensor_reduce(ss[s][:, t, :], sq[s][:, t, :].rearrange("p (h d) -> p h d", d=DH),
                                               AX_X, ALU.add))
                        dve.tensor_scalar(ss[s][:, t, :], ss[s][:, t, :], 1e-24, None,
                                          ALU.max).then_inc(ss_ready[s], 1)

                    def rotary_sum(t):
                        dve.wait_ge(qk_t[s], qk_t.at(k, l * TILES + t))
                        dve.tensor_tensor(t1[s][:, t, :], t1[s][:, t, :], t2[s][:, t, :],
                                          ALU.add).then_inc(qk_rot[s], 1)

                    yield
                    links[:] = own_attention, l * ATTENTION_LINKS
                    rotary_products(0)
                    yield
                    squared_norms(0)
                    yield
                    rotary_sum(0)
                    yield
                    rotary_products(1)
                    yield
                    normed_qk(0)
                    yield
                    squared_norms(1)
                    yield
                    rotary_sum(1)

                    def negated_max(u):
                        dve.wait_ge(s_ps[s], s_ps.at(k, l * UNITS + u))
                        sc = B4[:, u % 2, :].rearrange("p (e n) -> p e n", e=2)[:, :, keys(unit(u)[0])]
                        dve.tensor_reduce(nmax[s][:, u, :], sc, AX_X, ALU.max, negate=True).then_inc(mx_ready[s], 1)

                    def normed_out(t):
                        dve.wait_ge(pv_ps[s], pv_ps.at(k, l * UNITS + (t + 1) * PAIRS - 1))
                        link(dve.reciprocal(rsm[s][:, t, :], psm[s][:, t, :]))
                        dve.tensor_tensor(
                            o[s][:, t, :].rearrange("p (h d) -> p h d", d=DH),
                            B4[:, 3, :].rearrange("p (h d) -> p h d", d=DH),
                            rsm[s][:, t, :].unsqueeze(2).broadcast_to([P, HEADS, DH]),
                            ALU.mult).then_inc(o_sb[s], 1)

                    yield
                    negated_max(0)
                    for u in range(UNITS):
                        t, _ = unit(u)
                        j = l * UNITS + u
                        if u + 1 < UNITS:
                            yield
                            negated_max(u + 1)
                        if u == NORM_AT:
                            yield
                            normed_qk(1)
                        if u % 2 == 0:
                            yield
                            dve.wait_ge(pT_ps[s], pT_ps.at(k, j))
                            if u >= 2:
                                dve.wait_ge(pv_ps[s], pv_ps.at(k, j - 2))
                            src, dst = turned_probs(s, u)
                            dve.tensor_copy(dst, src).then_inc(pT_even[s], 1)
                        if u == PAIRS:
                            yield
                            normed_out(0)
                    yield
                    normed_out(1)
                    yield
                    dve.wait_ge(proj_ps[s], proj_ps.at(k, 1 + l))
                    pr = B4[:, 2, 0:TOK].rearrange("p (t n) -> p t n", t=TILES)
                    dve.tensor_tensor(h[s][:, :, :], h[s][:, :, :], pr, ALU.add).then_inc(h_mid[s], 1)

                def layer_ffn(l):
                    yield
                    links[:] = own_ffn, l * FFN_LINKS
                    dve.wait_ge(sh_ps[s], sh_ps.at(k, l))
                    dve.wait_ge(h_mid[s], h_mid.at(k, l))
                    second = B4[:, 3, 0:TILES * 64].rearrange("p (t n) -> p t n", t=TILES)
                    stats(lambda t: [h[s][:, t, 0:64], second[:, t, :]])
                    variance()
                    yield
                    dve.wait_ge(rstd_ready[s], rstd_ready.at(k, 3 + l))
                    for t in range(TILES):
                        normed(y[s][:, t, 0:64], h[s][:, t, 0:64], t)
                        ins = normed(y[s][:, t, 64:128], second[:, t, :], t)
                    ins.then_inc(hn_ready[s], 1)
                    for c, (_, n) in enumerate(HID_CHUNKS):
                        yield
                        dve.wait_ge(gate_sb[s], gate_sb.at(k, l * NCH + c))
                        dve.scalar_tensor_tensor(
                            out=hid[s][0:n, c, :], in0=B4[0:n, 1 + c, 0:TOK], scalar=b1f[0:n, l, 0, c:c + 1],
                            in1=gate[s][0:n, c, :], op0=ALU.add, op1=ALU.mult).then_inc(hid_sb[s], 1)
                    yield
                    dve.wait_ge(f2_ps[s], f2_ps.at(k, l))
                    fo = B4[:, 0, 0:TOK].rearrange("p (t n) -> p t n", t=TILES)
                    dve.tensor_tensor(h[s][:, :, :], h[s][:, :, :], fo, ALU.add).then_inc(h_ready[s], 1)

                def last_norm():
                    yield
                    links[:] = own_last, 0
                    dve.wait_ge(h_ready[s], h_ready.at(k, DEPTH))
                    stats(lambda t: [h[s][:, t, :]])
                    variance()
                    yield
                    dve.wait_ge(rstd_ready[s], rstd_ready.at(k, 3 + DEPTH))
                    link(*[normed(y[s][:, t, :], h[s][:, t, :], t) for t in range(TILES)])
                    yield
                    dve.wait_ge(s_st[s], k * 16 + 16)
                    dve.tensor_tensor(fin[s][:, :, :], x1[s][:, :, :], y[s][:, :, :],
                                      ALU.add).then_inc(fin_ready[s], 1)
                    assert links[1] == LAST_LINKS, links[1]

                return attention_block, layer_attention, layer_ffn, last_norm

            run_streams(dve, ROUNDS, "vector", parts)

        @block.tensor
        def _(pe):
            pe.wait_ge(s_raw, 16 * LOADS_TO_PREPARE)
            for l in range(DEPTH):
                for part in range(2):
                    for c, (c0, n) in enumerate(HID_CHUNKS):
                        col = (l * 2 + part) * NCH + c
                        ins = pe.matmul(ps[0][0:n, 0, col:col + 1],
                                        w1_raw[:, l, part * HID + c0:part * HID + c0 + n], lnb[:, l:l + 1],
                                        start=True, stop=True)
            ins.then_inc(s_wp, 1)
            pe.wait_ge(s_w, 16 * LOADS)
            pe.wait_ge(s_wa, 2)
            pe.wait_ge(s_wb, 2)
            pe.wait_ge(s_init, PRESETS)

            def parts(s, k):
                B4 = ps[s]

                def transpose4(dst, src):
                    for c in range(PAIRS):
                        ins = pe.transpose(dst[:, c * P:(c + 1) * P], src[:, c * P:(c + 1) * P], ident[:, :])
                    return ins

                def turn_out(n, t):
                    if n == 0:
                        pe.wait_ge(ao_sb[s], ao_sb.at(k, 1))
                    else:
                        pe.wait_ge(o_sb[s], o_sb.at(k, (n - 1) * TILES + t))
                    transpose4(B4[:, t, :], o[s][:, t, :]).then_inc(oT_ps[s], 1)

                def out_projection(n, w):
                    for t in range(TILES):
                        yield
                        pe.wait_ge(oT_sb[s], oT_sb.at(k, n * TILES + t))
                        for c in range(PAIRS):
                            ins = pe.matmul(B4[:, 2, t * P:(t + 1) * P], oT[s][:, c, t * P:(t + 1) * P],
                                            w[:, c, :], start=(c == 0), stop=(c == PAIRS - 1))
                    ins.then_inc(proj_ps[s], 1)

                def attention_block():
                    yield
                    pe.wait_ge(y_ready[s], y_ready.at(k, 0))
                    for t in range(TILES):
                        ins = pe.transpose(B4[:, 3, t * P:(t + 1) * P], y[s][:, t, :], ident[:, :])
                    ins.then_inc(act_ps[s], 1)
                    yield
                    pe.wait_ge(act_sb[s], act_sb.at(k, 0))
                    for t in range(TILES):
                        ins = pe.matmul(B4[:, 2, t * P:(t + 1) * P], actT[s][:, t * P:(t + 1) * P], wkv_s[:, :],
                                        start=True, stop=True)
                    ins.then_inc(aq_ps[s], 1)
                    for t in range(TILES):
                        pe.matmul(B4[:, t, :], actT[s][:, t * P:(t + 1) * P], wq_s[:, :],
                                  start=True, stop=True).then_inc(aq_ps[s], 1)
                    for t, bank in ((0, 3), (1, 0)):
                        yield
                        pe.wait_ge(aqk_n[s], aqk_n.at(k, t))
                        transpose4(B4[:, bank, :], qk[s][:, t, 0:INNER]).then_inc(aqT_ps[s], 1)
                    yield
                    pe.wait_ge(aqk_n[s], aqk_n.at(k, 2))
                    for t in range(TILES):
                        ins = pe.transpose(B4[:, 1, t * P:(t + 1) * P], qk[s][:, t, INNER:INNER + P], ident[:, :])
                    ins.then_inc(aqT_ps[s], 1)

                    def scores(hd):
                        if hd >= 2:
                            pe.wait_ge(ap_sb[s], ap_sb.at(k, hd - 2))
                        for kb in range(TILES):
                            ins = pe.matmul(B4[:, hd % 2, kb * TOK:(kb + 1) * TOK],
                                            kT[s][:, hd % 2, 0, kb * P:(kb + 1) * P], qT[s][:, hd // 2, :],
                                            start=True, stop=True)
                        ins.then_inc(as_ps[s], 1)

                    def values(hd):
                        pe.wait_ge(ap_sb[s], ap_sb.at(k, hd))
                        if hd == 4:
                            pe.wait_ge(ao_sb[s], ao_sb.at(k, 0))
                        cols = slice((hd % 4) * P, (hd % 4 + 1) * P)
                        for t in range(TILES):
                            for kb in range(TILES):
                                ins = pe.matmul(B4[:, 2 + t, cols], pb[s][hd % 2][:, kb, t * P:(t + 1) * P],
                                                v1[s][:, kb, :], start=(kb == 0), stop=(kb == TILES - 1))
                        ins.then_inc(ao_ps[s], 1)

                    yield
                    pe.wait_ge(aqT_sb[s], aqT_sb.at(k, 2))
                    pe.wait_ge(av_sb[s], av_sb.at(k, 0))
                    scores(0)
                    for hd in range(HEADS):
                        yield
                        if hd + 1 < HEADS:
                            scores(hd + 1)
                        yield
                        values(hd)
                    for t in range(TILES):
                        yield
                        turn_out(0, t)
                    yield from out_projection(0, wout_s)

                def layer_attention(l):
                    def project(t, part, bank):
                        return pe.matmul(B4[:, bank, :], shT[s][:, t * P:(t + 1) * P],
                                         wqkv_s[l][:, part * INNER:(part + 1) * INNER], start=True, stop=True)

                    yield
                    pe.wait_ge(h_ready[s], h_ready.at(k, l))
                    for t in range(TILES):
                        ins = pe.transpose(B4[:, 3, t * P:(t + 1) * P], h[s][:, t, :], ident[:, :])
                    ins.then_inc(act_ps[s], 1)
                    yield
                    pe.wait_ge(act_sb[s], act_sb.at(k, 1 + 2 * l))
                    project(0, 0, 0)
                    project(0, 1, 1).then_inc(qk_ps[s], 1)
                    for t in range(TILES):
                        project(t, 2, 2 + t).then_inc(v_ps[s], 1)
                    yield
                    pe.wait_ge(qk_t[s], qk_t.at(k, l * TILES))
                    project(1, 0, 0)
                    project(1, 1, 1).then_inc(qk_ps[s], 1)
                    yield
                    pe.wait_ge(qk_n[s], qk_n.at(k, l * TILES))
                    for part in range(2):
                        pe.wait_ge(v_sb[s], v_sb.at(k, l * TILES + part))
                        transpose4(B4[:, 2 + part, :],
                                   qk[s][:, 0, part * INNER:(part + 1) * INNER]).then_inc(qkT_ps[s], 1)

                    def scores(u):
                        t, heads = unit(u)
                        if u >= 2:
                            pe.wait_ge(p_sb[s], p_sb.at(k, l * UNITS + u - 2))
                        kk = keys(t)
                        sc = B4[:, u % 2, :].rearrange("p (e n) -> p e n", e=2)
                        pe.matmul(sc[:, :, kk], identb[:, :],
                                  maskb[:, t, kk].unsqueeze(1).broadcast_to([P, 2, kk.stop - kk.start]),
                                  start=True, stop=False)
                        for e, hd in enumerate(heads):
                            ins = pe.matmul(sc[:, e, kk], qT[s][:, hd // 2, t * P:(t + 1) * P],
                                            kT[s][:, hd % 2, hd // 2, kk], start=False, stop=(e == 1))
                        ins.then_inc(s_ps[s], 1)

                    def turn(u):
                        t, _ = unit(u)
                        j = l * UNITS + u
                        pe.wait_ge(p_sb[s], p_sb.at(k, j))
                        if u % 2:
                            pe.wait_ge(pT_even[s], pT_even.at(k, j // 2))
                        elif u:
                            pe.wait_ge(pT_odd[s], pT_odd.at(k, j // 2 - 1))
                        nb = len(blocks(t))
                        for e in range(2):
                            for b in blocks(t):
                                ins = pe.transpose(B4[:, 2, (e * nb + b) * P:(e * nb + b + 1) * P],
                                                   pb[s][2 * t + u % 2][:, e, b * P:(b + 1) * P], ident[:, :])
                        ins.then_inc(pT_ps[s], 1)

                    def values(u):
                        t, heads = unit(u)
                        pT_sb = pT_odd if u % 2 else pT_even
                        pe.wait_ge(pT_sb[s], pT_sb.at(k, (l * UNITS + u) // 2))
                        if u == PAIRS:
                            pe.wait_ge(o_sb[s], o_sb.at(k, l * TILES))
                        for e, hd in enumerate(heads):
                            for b in blocks(t):
                                ins = pe.matmul(B4[:, 3, hd * DH:(hd + 1) * DH], pT[s][u % 2][:, e, b, :],
                                                v8[s][:, b, hd * DH:(hd + 1) * DH],
                                                start=(b == 0), stop=(b == t))
                        ins.then_inc(pv_ps[s], 1)

                    yield
                    pe.wait_ge(qkT_sb[s], qkT_sb.at(k, l * TILES * 2 + 1))
                    pe.wait_ge(qk_t[s], qk_t.at(k, l * TILES + 1))
                    scores(0)
                    scores(1)
                    for u in range(UNITS):
                        yield
                        turn(u)
                        if u + 2 == TURN_AT:
                            yield
                            pe.wait_ge(qk_n[s], qk_n.at(k, l * TILES + 1))
                            for part in range(2):
                                pe.wait_ge(p_sb[s], p_sb.at(k, l * UNITS + u + part))
                                transpose4(B4[:, part, :],
                                           qk[s][:, 1, part * INNER:(part + 1) * INNER]).then_inc(qkT_ps[s], 1)
                        if u + 2 == TURN_AT:
                            yield
                            pe.wait_ge(qkT_sb[s], qkT_sb.at(k, l * TILES * 2 + 3))
                        if u + 2 < UNITS:
                            scores(u + 2)
                        if u:
                            yield
                            values(u - 1)
                    yield
                    turn_out(1 + l, 0)
                    yield
                    values(UNITS - 1)
                    yield
                    turn_out(1 + l, 1)
                    yield from out_projection(1 + l, wo_s[l])

                def layer_ffn(l):
                    yield
                    pe.wait_ge(h_mid[s], h_mid.at(k, l))
                    for t in range(TILES):
                        dst = B4[:, 3, t * 64:(t + 1) * 64]
                        ins = pe.matmul(dst, shift[:, 0, :], h[s][:, t, 64:128], start=True, stop=(t == 0))
                        if t:
                            ins = pe.matmul(dst, shift[:, 1, :], h[s][:, t - 1, 64:128], start=False, stop=True)
                    ins.then_inc(sh_ps[s], 1)
                    yield
                    pe.wait_ge(hn_ready[s], hn_ready.at(k, l))
                    for t in range(TILES):
                        ins = pe.transpose(B4[:, 0, t * P:(t + 1) * P], y[s][:, t, :], ident[:, :])
                    ins.then_inc(act_ps[s], 1)
                    yield
                    pe.wait_ge(act_sb[s], act_sb.at(k, 2 + 2 * l))
                    for c, (c0, n) in enumerate(HID_CHUNKS):
                        for part in range(2):
                            ins = pe.matmul(B4[0:n, 1 + c, part * TOK:(part + 1) * TOK],
                                            w1_s[l][:, part * HID + c0:part * HID + c0 + n],
                                            actT[s][:, 0:TOK], start=True, stop=True)
                        ins.then_inc(f1_ps[s], 1)
                    yield
                    for t in range(TILES):
                        for c, (_, n) in enumerate(HID_CHUNKS):
                            yield
                            pe.wait_ge(hid_sb[s], hid_sb.at(k, l * NCH + c))
                            n += c == NCH - 1
                            ins = pe.matmul(B4[:, 0, t * P:(t + 1) * P], hid[s][0:n, c, t * P:(t + 1) * P],
                                            w2_s[l][0:n, c, :], start=(c == 0), stop=(c == NCH - 1))
                    ins.then_inc(f2_ps[s], 1)

                return attention_block, layer_attention, layer_ffn, nothing

            run_streams(pe, ROUNDS, "tensor", parts)


def nothing():
    return iter(())


TURNS = {
    "gpsimd": (2, (
        "010011110000111100011100"
    )),
    "scalar": (4, (
        "0000111100000001110010011001111100011011000100100000001010100101010111111101000110101110"
        "001100100000001011101010010101011011111111110111000111"
    )),
    "vector": (9, (
        "0011000001111111110111110000100000100000000100110000110101101101101111010001101110100100"
        "1000010000101011101000101101101111011110110111111000100010"
    )),
    "tensor": (10, (
        "1001101001011111000000010100000000110100011111111010110111111010110001000000010100100000"
        "0100010111110010010010001011011011111101101001000010110111111010010010000001001011101111"
        "110111101111000110000111"
    )),
}


def head(attention_block, layer_attention, layer_ffn, last_norm):
    yield from attention_block()
    for l in range(DEPTH - 1):
        yield from layer_attention(l)
        yield from layer_ffn(l)
    yield from layer_attention(DEPTH - 1)


def tail(attention_block, layer_attention, layer_ffn, last_norm):
    yield from layer_ffn(DEPTH - 1)
    yield from last_norm()


def interleave(turns, *programs):
    done = object()
    for steps in programs:
        next(steps)
    taken = [next(programs[int(s)], done) for s in turns]
    assert taken.count(done) == len(programs), "steps without a turn"


def run_streams(eng, rounds, name, parts):
    tail_steps, turns = TURNS[name]
    seen = 0
    first_turns = ""
    for s in turns:
        seen += s == "1"
        if s == "0" or seen > tail_steps:
            first_turns += s
    first = parts(0, 0)
    interleave(first_turns, chain(head(*first), tail(*first)), head(*parts(1, 0)))
    with eng.Fori(1, rounds) as k:
        mine = parts(0, k)
        interleave(turns, chain(head(*mine), tail(*mine)), chain(tail(*parts(1, k - 1)), head(*parts(1, k))))
    for _ in tail(*parts(1, rounds - 1)):
        pass




_INS = ['L0_attn_x', 'L0_attn_norm_g', 'L0_attn_Wq', 'L0_attn_Wkv', 'L0_attn_Wout', 'L0_attn_out_norm_g',
        'L0_ffn_wqkv', 'L0_ffn_q_scale', 'L0_ffn_k_scale', 'L0_ffn_wo', 'L0_ffn_ln_g', 'L0_ffn_ln_b',
        'L0_ffn_w1', 'L0_ffn_b1', 'L0_ffn_w2', 'L0_ffn_b2']
_OUTS = [((16, 256, 128), 'float32')]


def kernel(**inputs):
    import numpy as _np
    import concourse.bacc as _bacc
    from concourse import mybir as _mybir
    from concourse.bass_utils import run_bass_kernel_spmd as _run

    nc = _bacc.Bacc("TRN2", target_bir_lowering=False, num_devices=1)
    given = {name: _np.ascontiguousarray(inputs[name]) for name in _INS}
    given.update(shape_constants())
    arrays, args = {}, []
    for name, a in given.items():
        arrays[f"in_{name}_dram"] = a
        args.append(nc.dram_tensor(f"in_{name}_dram", a.shape, _mybir.dt.from_np(a.dtype), kind="ExternalInput").ap())
    for i, (shape, dtype) in enumerate(_OUTS):
        dt = _mybir.dt.from_np(_np.dtype(dtype))
        args.append(nc.dram_tensor(f"out_{i}_dram", shape, dt, kind="ExternalOutput").ap())
    sandwich_kernel(nc, *args)
    r = _run(nc, [arrays], core_ids=[0])
    got = tuple(r.results[0][f"out_{i}_dram"] for i in range(len(_OUTS)))
    return got[0]
```
